# Optimizing a Trainium2 kernel written in Bass

```python
import numpy as np
import jax
import jax.numpy as jnp

def _softmax(x, axis=-1):
    return jax.nn.softmax(x, axis=axis)

def _gelu(x):
    return jax.nn.gelu(x, approximate=True)

def _silu(x):
    return jax.nn.silu(x)

def _sigmoid(x):
    return jax.nn.sigmoid(x)

def _layernorm(x, axis=-1, eps=1e-05):
    m = jnp.mean(x, axis=axis, keepdims=True)
    v = jnp.var(x, axis=axis, keepdims=True)
    return (x - m) / jnp.sqrt(v + eps)

def _scatter_add(tgt, idx, src, axis=0):
    return tgt.at[idx].add(src)

def _segment_sum(src, seg, n):
    return jax.ops.segment_sum(src, seg, n)
kernel_name = 'mk_adj_resnorm_d4_adj_r2_1ef789'

def setup_inputs(seed: int=0):
    np.random.seed(seed)
    _w = jnp.asarray

    def _rec_inputs():
        import jax
        import jax.numpy as jnp
        _gk = jax.random.key(seed)
        x = -0.000929 + 1 * jax.random.normal(jax.random.fold_in(_gk, 1), (4096, 128), jnp.float32)
        _a = jax.random.bernoulli(jax.random.fold_in(_gk, 2), 0.00195312, (4096, 4096))
        _a = jnp.logical_or(_a, jnp.swapaxes(_a, -1, -2))
        _a = jnp.logical_or(_a, jnp.eye(4096, dtype=bool))
        _af = _a.astype(jnp.float32)
        _af = _af * jax.random.uniform(jax.random.fold_in(_gk, 3), (4096, 4096), jnp.float32, 0.05, 0.0598829)
        adj = _af
        return (x, adj)
    x, adj = _rec_inputs()

    def _L0_gnn_setup():
        import jax, jax.numpy as jnp
        import numpy as np
        N, F_DIM, H_DIM = (4096, 128, 128)

        def _gwnn_layer(features, wavelets, wavelets_inv, W, filt):
            xw = features @ W
            spec = wavelets_inv @ xw
            spec = filt[:, None] * spec
            return wavelets @ spec
        key = jax.random.key(seed)
        ks = jax.random.split(key, 7)
        inp = {'input': jax.random.normal(ks[0], (N, F_DIM), dtype=jnp.float32), 'wavelets': jax.random.normal(ks[1], (N, N), dtype=jnp.float32) / np.sqrt(N), 'wavelets_inv': jax.random.normal(ks[2], (N, N), dtype=jnp.float32) / np.sqrt(N), 'W1': jax.random.uniform(ks[3], (F_DIM, H_DIM), dtype=jnp.float32, minval=-np.sqrt(6.0 / (F_DIM + H_DIM)), maxval=np.sqrt(6.0 / (F_DIM + H_DIM))), 'f1': jax.random.uniform(ks[4], (N,), dtype=jnp.float32, minval=0.9, maxval=1.1), 'W2': jax.random.uniform(ks[5], (H_DIM, H_DIM), dtype=jnp.float32, minval=-np.sqrt(6.0 / (H_DIM + H_DIM)), maxval=np.sqrt(6.0 / (H_DIM + H_DIM))), 'f2': jax.random.uniform(ks[6], (N,), dtype=jnp.float32, minval=0.9, maxval=1.1)}
        return inp
    _L0_gnn_all = _L0_gnn_setup()
    _L0_gnn_in = {k: v for k, v in _L0_gnn_all.items() if k in ('W1', 'f1', 'W2', 'f2')}
    del _L0_gnn_all

    def _L1_gnn_setup():
        import jax, jax.numpy as jnp
        import numpy as np
        N = 8192
        F_IN = 128
        F_OUT = 128
        key = jax.random.key(seed)
        k1, k2, k3 = jax.random.split(key, 3)
        x = jax.random.normal(k1, (N, F_IN), dtype=jnp.float32)
        adj = jax.random.uniform(k2, (N, N), dtype=jnp.float32)
        stdv = 1.0 / np.sqrt(F_OUT)
        w = jax.random.uniform(k3, (2 * F_IN, F_OUT), dtype=jnp.float32, minval=-stdv, maxval=stdv)
        return {'input': x, 'adj': adj, 'weight': w}
    _L1_gnn_all = _L1_gnn_setup()
    _L1_gnn_in = {k: v for k, v in _L1_gnn_all.items() if k in ('weight',)}
    del _L1_gnn_all

    def _L2_gnn_setup():
        import jax, jax.numpy as jnp
        import numpy as np
        import math
        N = 4096
        D_IN = 128
        H = 128
        GATE_TEMPERATURE = 1.0
        LN_EPS = 1e-05
        key = jax.random.key(seed)
        ks = jax.random.split(key, 10)
        s_msg = 1.0 / math.sqrt(D_IN)
        s_gate = 1.0 / math.sqrt(H)
        s_upd = 1.0 / math.sqrt(D_IN + H)
        return {'node_features': jax.random.normal(ks[0], (N, D_IN), dtype=jnp.float32), 'adj_matrix': jax.random.uniform(ks[1], (N, N), dtype=jnp.float32), 'recency_prior': jax.random.uniform(ks[2], (N, N), dtype=jnp.float32), 'W_msg': jax.random.uniform(ks[3], (D_IN, H), jnp.float32, -s_msg, s_msg), 'b_msg': jax.random.uniform(ks[4], (H,), jnp.float32, -s_msg, s_msg), 'W_q': jax.random.uniform(ks[5], (H, H), jnp.float32, -s_gate, s_gate), 'W_k': jax.random.uniform(ks[6], (H, H), jnp.float32, -s_gate, s_gate), 'gate_bias': jnp.float32(-1.0), 'W_upd': jax.random.uniform(ks[7], (D_IN + H, H), jnp.float32, -s_upd, s_upd), 'b_upd': jax.random.uniform(ks[8], (H,), jnp.float32, -s_upd, s_upd), 'ln_gamma': jnp.ones((H,), jnp.float32), 'ln_beta': jnp.zeros((H,), jnp.float32)}
    _L2_gnn_all = _L2_gnn_setup()
    _L2_gnn_in = {k: v for k, v in _L2_gnn_all.items() if k in ('W_msg', 'b_msg', 'W_q', 'W_k', 'gate_bias', 'W_upd', 'b_upd', 'ln_gamma', 'ln_beta')}
    del _L2_gnn_all

    def _L3_gnn_setup():
        import jax, jax.numpy as jnp
        import numpy as np
        N = 8192
        U = 128
        AVG_DEGREE = 32
        key = jax.random.key(seed)
        kx, ka, kw = jax.random.split(key, 3)
        x = jax.random.normal(kx, (N, U), dtype=jnp.float32)
        adj = (jax.random.uniform(ka, (N, N)) < AVG_DEGREE / N).astype(jnp.float32)
        W = jax.random.normal(kw, (U, U), dtype=jnp.float32) * 0.05
        b = jnp.zeros((U,), dtype=jnp.float32)
        return {'x': x, 'adj': adj, 'W': W, 'b': b}
    _L3_gnn_all = _L3_gnn_setup()
    _L3_gnn_in = {k: v for k, v in _L3_gnn_all.items() if k in ('W', 'b')}
    del _L3_gnn_all
    return {'x': x, 'adj': adj, 'L0_gnn_W1': _L0_gnn_in['W1'], 'L0_gnn_f1': _L0_gnn_in['f1'], 'L0_gnn_W2': _L0_gnn_in['W2'], 'L0_gnn_f2': _L0_gnn_in['f2'], 'L1_gnn_weight': _L1_gnn_in['weight'], 'L2_gnn_W_msg': _L2_gnn_in['W_msg'], 'L2_gnn_b_msg': _L2_gnn_in['b_msg'], 'L2_gnn_W_q': _L2_gnn_in['W_q'], 'L2_gnn_W_k': _L2_gnn_in['W_k'], 'L2_gnn_gate_bias': _L2_gnn_in['gate_bias'], 'L2_gnn_W_upd': _L2_gnn_in['W_upd'], 'L2_gnn_b_upd': _L2_gnn_in['b_upd'], 'L2_gnn_ln_gamma': _L2_gnn_in['ln_gamma'], 'L2_gnn_ln_beta': _L2_gnn_in['ln_beta'], 'L3_gnn_W': _L3_gnn_in['W'], 'L3_gnn_b': _L3_gnn_in['b']}

def reference(x, adj, L0_gnn_W1, L0_gnn_f1, L0_gnn_W2, L0_gnn_f2, L1_gnn_weight, L2_gnn_W_msg, L2_gnn_b_msg, L2_gnn_W_q, L2_gnn_W_k, L2_gnn_gate_bias, L2_gnn_W_upd, L2_gnn_b_upd, L2_gnn_ln_gamma, L2_gnn_ln_beta, L3_gnn_W, L3_gnn_b):
    import jax
    import jax.numpy as jnp

    def _L0_gnn_ref(input, wavelets, wavelets_inv, W1, f1, W2, f2):
        import jax, jax.numpy as jnp
        import numpy as np
        N, F_DIM, H_DIM = (4096, 128, 128)

        def _gwnn_layer(features, wavelets, wavelets_inv, W, filt):
            xw = features @ W
            spec = wavelets_inv @ xw
            spec = filt[:, None] * spec
            return wavelets @ spec
        h1 = jax.nn.relu(_gwnn_layer(input, wavelets, wavelets_inv, W1, f1))
        out = _gwnn_layer(h1, wavelets, wavelets_inv, W2, f2)
        return out

    def _L1_gnn_ref(input, adj, weight):
        import jax, jax.numpy as jnp
        import numpy as np
        N = 8192
        F_IN = 128
        F_OUT = 128
        support = adj @ input
        h = jnp.concatenate([input, support], axis=1)
        return h @ weight

    def _L2_gnn_ref(node_features, adj_matrix, recency_prior, W_msg, b_msg, W_q, W_k, gate_bias, W_upd, b_upd, ln_gamma, ln_beta):
        import jax, jax.numpy as jnp
        import numpy as np
        import math
        N = 4096
        D_IN = 128
        H = 128
        GATE_TEMPERATURE = 1.0
        LN_EPS = 1e-05
        messages = node_features @ W_msg + b_msg
        q = messages @ W_q
        k = messages @ W_k
        scale = math.sqrt(H) * max(GATE_TEMPERATURE, 1e-06)
        logits = q @ k.T / scale + gate_bias
        probs = jax.nn.sigmoid(logits)
        gates_masked = probs * adj_matrix * recency_prior
        aggregated = gates_masked @ messages
        updated = jnp.concatenate([node_features, aggregated], axis=1) @ W_upd + b_upd
        updated = jax.nn.relu(updated)
        mu = jnp.mean(updated, axis=-1, keepdims=True)
        var = jnp.var(updated, axis=-1, keepdims=True)
        out = (updated - mu) * jax.lax.rsqrt(var + LN_EPS) * ln_gamma + ln_beta
        return out

    def _L3_gnn_ref(x, adj, W, b):
        import jax, jax.numpy as jnp
        import numpy as np
        N = 8192
        U = 128
        AVG_DEGREE = 32
        adj = jax.lax.stop_gradient(adj)
        neigh1 = adj @ x
        x1 = jax.nn.swish(neigh1 @ W + b)
        neigh2 = adj @ x1
        x2 = jax.nn.swish(neigh2 @ W + b)
        return x2
    x = _layernorm(x + _L0_gnn_ref(x, adj, adj, L0_gnn_W1, L0_gnn_f1, L0_gnn_W2, L0_gnn_f2), axis=-1)
    x = _layernorm(x + _L1_gnn_ref(x, adj, L1_gnn_weight), axis=-1)
    x = _layernorm(x + _L2_gnn_ref(x, adj, adj, L2_gnn_W_msg, L2_gnn_b_msg, L2_gnn_W_q, L2_gnn_W_k, L2_gnn_gate_bias, L2_gnn_W_upd, L2_gnn_b_upd, L2_gnn_ln_gamma, L2_gnn_ln_beta), axis=-1)
    x = _layernorm(x + _L3_gnn_ref(x, adj, L3_gnn_W, L3_gnn_b), axis=-1)
    return x

_drawn_inputs = setup_inputs


def setup_inputs(seed=0):
    import zlib

    import numpy as np

    out = dict(_drawn_inputs(seed))
    spreads = {'L2_gnn_ln_gamma': (1.0, 0.2), 'L2_gnn_ln_beta': (0.0, 0.1), 'L3_gnn_b': (0.0, 0.1)}
    factors = {'L0_gnn_W1': 4.282,
     'L0_gnn_f1': 200.0,
     'L0_gnn_f2': 200.0,
     'L2_gnn_W_msg': 8.0,
     'L2_gnn_b_msg': 200.0,
     'L2_gnn_W_q': 38.594,
     'L2_gnn_W_k': 8.0,
     'L3_gnn_W': 3.314}
    for name, (base, spread) in spreads.items():
        noise = np.random.default_rng([zlib.crc32(name.encode()), seed]).standard_normal(out[name].shape)
        drawn = base * np.exp(spread * noise) if base else spread * noise
        out[name] = jnp.asarray(drawn.astype(out[name].dtype))
    for name, factor in factors.items():
        out[name] = (out[name] * factor).astype(out[name].dtype)
    return out
```

```python
from collections import namedtuple
from contextlib import ExitStack

import concourse.bass as bass
from concourse import mybir

P = 128
N = 4096
F = 128
NB = N // P
CH = 1024
NC = N // CH
CB = CH // P
SJ = 2
STEPS = NB // SJ
RING = 4
BANK = 512
HALVES = CH // BANK
PASSES = 8
GATED = 6
AHEAD = 2

A_EXP = 10
G_EXP = 12
Y_EXP = [3, -2, 0, -5, 5, 2, 5, 5]
Q_EXP, K_EXP = 0, 2
LN_EPS = 1e-5
NEWTON = 3

ALU = mybir.AluOpType
ACT = mybir.ActivationFunctionType
AX = mybir.AxisListType.X
F32 = mybir.dt.float32
F16 = mybir.dt.float16

PER_CHUNK = {
    "x_T": {4: 1, 5: 1},
    "rows": {0: 1, 1: 1, 2: 1, 3: 1, 4: 2, 5: 6, 6: 1, 7: 1, 8: 1},
    "zt": {p: 1 for p in range(1, 9)},
    "val": {1: 1, 3: 1, 4: 1, 5: 1, 6: 1, 7: 1, 8: 1},
    "nonlin": {6: 1, 7: 1, 8: 1},
    "swished": {7: 1, 8: 1},
    "resid": {8: 1},
    "affine": {6: 3},
    "ln": {4: 1, 5: 1, 6: 2, 8: 1},
    "yhi": {p: 1 for p in range(0, 8)},
    "ylo": {p: 1 for p in range(0, 8)},
    "msg": {5: 1},
    "qk": {5: 2},
    "xsave": {4: 1, 5: 1, 6: 1, 8: 1},
}


def nth(stage, p, ic, k=0):
    per = PER_CHUNK[stage]
    return NC * sum(n for q, n in per.items() if q < p) + per[p] * ic + k + 1


def plain_chunk(p, ic):
    return NC * (p - 1 if p < GATED else p - 2) + ic


Chunk = namedtuple("Chunk", "p ic src half buf level")


def build(nc, adj, x, xt, W1, f1, W2, f2, Wcat, W_msg, b_msg, W_q, W_k, gate_bias, W_upd, b_upd, ln_g, ln_b, W3, b3, out):
    with ExitStack() as ctx:
        def sb(name, shape, dt=F32):
            return ctx.enter_context(nc.sbuf_tensor(name, shape, dt))

        def sem(name):
            return ctx.enter_context(nc.semaphore(name))

        a_ring = sb("a_ring", [P, RING, SJ, CH])
        a_hi = sb("a_hi", [P, RING, SJ, CH], F16)
        a_lo = sb("a_lo", [P, RING, SJ, CH], F16)
        y_hi = sb("y_hi", [P, 2, N], F16)
        y_lo = sb("y_lo", [P, 2, N], F16)
        x_rows = sb("x_rows", [P, NB, F])
        x_T = sb("x_T", [P, N])
        qT_hi, qT_lo = sb("qT_hi", [P, N], F16), sb("qT_lo", [P, N], F16)
        kT_hi, kT_lo = sb("kT_hi", [P, N], F16), sb("kT_lo", [P, N], F16)
        gates = sb("gates", [P, 2, CH])
        a_sq = sb("a_sq", [P, 2, CH])
        z_T = sb("z_T", [P, CH])
        val = sb("val", [P, CB, F])
        tmp = sb("tmp", [P, CB, F])
        m_T = tmp[:, :, :].rearrange("p b f -> p (b f)")
        xn = sb("xn", [P, CB, F])
        stats = sb("stats", [P, 8, CB])
        ident = sb("ident", [P, P])
        w1, w2, w3 = sb("w1", [P, F]), sb("w2", [P, F]), sb("w3", [P, F])
        wcat, wupd = sb("wcat", [P, 2, F]), sb("wupd", [P, 2, F])
        wmsg, wq, wk = sb("wmsg", [P, F]), sb("wq", [P, F]), sb("wk", [P, F])
        f1c, f2c = sb("f1c", [P, NB]), sb("f2c", [P, NB])
        bmsg, gbias = sb("bmsg", [P, 1]), sb("gbias", [P, 1])
        bupd, gam, bet, b3r = sb("bupd", [P, F]), sb("gam", [P, F]), sb("bet", [P, F]), sb("b3r", [P, F])

        acc = ctx.enter_context(nc.psum_tensor("acc", [P, 2, CH], F32))
        logits = ctx.enter_context(nc.psum_tensor("logits", [P, CH], F32))
        rows = ctx.enter_context(nc.psum_tensor("rows", [P, CB, F], F32))
        rows_flat = rows[:, :, :].rearrange("p b f -> p (b f)")

        s_small = sem("small_loaded")
        s_xt = sem("xt_loaded")
        s_a = [sem(f"a_loaded{i}") for i in range(RING)]
        s_id0, s_id = sem("ident_zero"), sem("ident_ready")
        s_ahi, s_alo, s_mm = sem("a_hi_ready"), sem("a_lo_ready"), sem("step_multiplied")
        s_lg, s_pr, s_sq = sem("logits_ready"), sem("probs_ready"), sem("a_sq_ready")
        s_g, s_ghi, s_glo, s_gm = sem("gates_ready"), sem("g_hi_ready"), sem("g_lo_ready"), sem("gates_multiplied")
        s_rows, s_xT = sem("rows_written"), sem("x_T_saved")
        s_zt, s_val, s_nl, s_sw = sem("z_T_ready"), sem("val_ready"), sem("nonlinearity_done"), sem("swish_done")
        s_res, s_aff = sem("residual_added"), sem("affine_done")
        s_sum, s_mean, s_cen, s_sqr = sem("ln_sum"), sem("ln_mean"), sem("ln_centred"), sem("ln_squared")
        s_ss, s_var, s_rstd, s_ln = sem("ln_sum_sq"), sem("ln_var"), sem("ln_rstd"), sem("ln_done")
        s_root, s_inv, s_newton = sem("ln_root"), sem("ln_inverse"), sem("ln_newton")
        s_yhi, s_y = sem("y_hi_ready"), sem("y_ready")
        s_msg, s_qkhi, s_qk = sem("m_T_ready"), sem("qk_hi_ready"), sem("qk_ready")
        s_xs, s_out = sem("x_saved"), sem("out_stored")

        small = [(x_rows[:, :, :], x), (w1[:], W1), (w2[:], W2), (w3[:], W3), (wmsg[:], W_msg), (wq[:], W_q),
                 (wk[:], W_k), (wcat[:, :, :], Wcat.rearrange("(t k) n -> k t n", t=2)),
                 (wupd[:, :, :], W_upd.rearrange("(t k) n -> k t n", t=2)), (f1c[:], f1), (f2c[:], f2),
                 (bmsg[:], b_msg.rearrange("(k a) -> k a", a=1)), (gbias[:], gate_bias.partition_broadcast(P)),
                 (bupd[:], b_upd.partition_broadcast(P)), (gam[:], ln_g.partition_broadcast(P)),
                 (bet[:], ln_b.partition_broadcast(P)), (b3r[:], b3.partition_broadcast(P))]
        SMALL = 16 * len(small)

        def blk(t, b):
            return t[:, b * P:(b + 1) * P]

        def over_blocks(v):
            return v[:, :].unsqueeze(1).to_broadcast([P, CB, F])

        def over_features(v):
            return v.unsqueeze(2).to_broadcast([P, CB, F])

        def x_chunk(ic):
            return x_rows[:, bass.ds(ic * CB, CB), :]

        def schedule(eng, plain, gated, stages, lead, gated_lead):
            def stream(at, ended):
                first = gated_lead if at.p == GATED else lead
                step = gated if at.p == GATED else plain
                for jp in range(STEPS):
                    epilogue = [(op, ended) for op in (stages(ended.p).get(jp - first, []) if ended else [])]
                    if step:
                        step(at, jp, epilogue)
                    else:
                        run(epilogue)

            def static(p, ic):
                return Chunk(p, ic, ic, ic % 2, (p - 1) % 2, p - 1)

            stream(static(1, 0), None)
            for p in range(1, PASSES + 1):
                if p in (GATED - 1, GATED, PASSES):
                    for ic in range(1, NC):
                        stream(static(p, ic), static(p, ic - 1))
                    if p < PASSES:
                        stream(static(p + 1, 0), static(p, NC - 1))
                elif plain or stages(p):
                    with eng.Fori(0, NC // 2) as r:
                        buf = (p - 1) % 2
                        even, odd = Chunk(p, 2 * r, None, 0, buf, p - 1), Chunk(p, 2 * r + 1, 2 * r + 1, 1, buf, p - 1)
                        after = Chunk(p, 2 * r + 2, r * -2 + 2, 0, r * -1 + 1 if buf else r, p - 1 + r)
                        stream(odd, even)
                        stream(after, odd)
            for tau in sorted(stages(PASSES)):
                run([(op, static(PASSES, NC - 1)) for op in stages(PASSES)[tau]])

        def after_gated(at):
            return at.p == GATED + 1 and isinstance(at.ic, int) and at.ic == 0

        def run(epilogue):
            for op, ended in epilogue:
                op(ended)

        block = ctx.enter_context(nc.Block())

        @block.sync
        def _(sp):
            sp.dma_start(x_T[:, :], xt).then_inc(s_xt, 16)

            def load(at, jp):
                sp.dma_start(a_ring[:, jp % RING, :, :],
                             adj[bass.ds(at.src, 1), jp].rearrange("o p s c -> (o p) s c")
                             ).then_inc(s_a[jp % RING], 16)

            def plain(at, jp, epilogue):
                n = STEPS * plain_chunk(at.p, at.ic) + jp
                if after_gated(at) and jp < RING:
                    sp.wait_ge(s_sq, NB * NC - SJ * RING + SJ * (jp + 1))
                elif not (isinstance(n, int) and n < RING):
                    sp.wait_ge(s_alo, n - RING + 1)
                load(at, jp)
                run(epilogue)

            def gated(at, jp, epilogue):
                n = STEPS * at.ic + jp
                if n < RING:
                    sp.wait_ge(s_alo, STEPS * plain_chunk(GATED - 1, NC) + jp - RING + 1)
                else:
                    sp.wait_ge(s_sq, SJ * (n - RING + 1))
                load(at, jp)
                run(epilogue)

            def store(ended):
                p, ic = ended.p, ended.ic
                sp.wait_ge(s_xs, nth("xsave", p, ic))
                sp.dma_start(out[:, ic * CB:(ic + 1) * CB, :], x_rows[:, ic * CB:(ic + 1) * CB, :]).then_inc(s_out, 16)

            schedule(sp, plain, gated, lambda p: {12: [store]} if p == PASSES else {}, 3, 1)
            sp.wait_ge(s_out, 16 * NC)

        @block.tensor
        def _(pe):
            def write_rows(products):
                products().then_inc(s_rows, 1)

            def transposes(source):
                def go():
                    for b in range(CB):
                        last = pe.transpose(rows[:, b, :], source(b), ident[:, :])
                    return last
                return go

            def by_node(*terms):
                def go():
                    for b in range(CB):
                        for t, (left, right) in enumerate(terms):
                            last = pe.matmul(rows[:, b, :], left(b), right, start=(t == 0), stop=(t == len(terms) - 1))
                    return last
                return go

            def by_feature(weight, right):
                def go():
                    for h in range(HALVES):
                        last = pe.matmul(rows_flat[:, h * BANK:(h + 1) * BANK], weight, right[:, h * BANK:(h + 1) * BANK],
                                         start=True, stop=True)
                    return last
                return go

            def project(ended):
                p, ic = ended.p, ended.ic
                pe.wait_ge(s_zt, nth("zt", p, ic))
                z = lambda b: blk(z_T, b)
                xT = lambda b: blk(x_T, ic * CB + b)
                terms = {1: transposes(z), 3: transposes(z), 4: transposes(z), 2: by_node((z, w2[:])),
                         7: by_node((z, w3[:])), 8: by_node((z, w3[:]))}
                if p == 5:
                    terms[5] = by_node((xT, wcat[:, 0, :]), (z, wcat[:, 1, :]))
                if p == 6:
                    terms[6] = by_node((xT, wupd[:, 0, :]), (z, wupd[:, 1, :]))
                write_rows(terms[p])

            def x_transposes(ended):
                p, ic = ended.p, ended.ic
                pe.wait_ge(s_ln, nth("ln", p, ic))
                write_rows(transposes(lambda b: xn[:, b, :]))

            def messages(ended):
                p, ic = ended.p, ended.ic
                pe.wait_ge(s_xT, nth("x_T", p, ic))
                write_rows(by_feature(wmsg[:], x_T[:, ic * CH:(ic + 1) * CH]))

            def queries(ended):
                p, ic = ended.p, ended.ic
                pe.wait_ge(s_msg, nth("msg", p, ic))
                write_rows(by_feature(wq[:], m_T))

            def keys(ended):
                p, ic = ended.p, ended.ic
                pe.wait_ge(s_qk, nth("qk", p, ic, 0))
                write_rows(by_feature(wk[:], m_T))

            def message_rows(ended):
                p, ic = ended.p, ended.ic
                pe.wait_ge(s_qk, nth("qk", p, ic, 1))
                write_rows(transposes(lambda b: blk(m_T, b)))

            def stages(p):
                s = {1: [project]}
                if p == 4:
                    s[4] = [x_transposes]
                if p == 5:
                    s.update({4: [x_transposes], 5: [messages], 6: [queries], 7: [keys], 8: [message_rows]})
                return s

            def product(at, jp, s):
                j = jp * SJ + s
                for t, (y, a) in enumerate([(y_hi, a_hi), (y_hi, a_lo), (y_lo, a_hi)]):
                    for h in range(HALVES):
                        mm = pe.matmul(acc[:, at.half, h * BANK:(h + 1) * BANK],
                                       y[:, bass.ds(at.buf, 1), j * P:(j + 1) * P].rearrange("p o f -> p (o f)"),
                                       a[:, jp % RING, s, h * BANK:(h + 1) * BANK],
                                       start=(j == 0 and t == 0), stop=(j == NB - 1 and t == 2))
                return mm

            def chunk_start(at, jp):
                g = NC * (at.p - 1) + at.ic
                if jp == 0 and not (isinstance(g, int) and g < 2):
                    pe.wait_ge(s_zt, g - 1)
                if jp % (CB // SJ) == 0:
                    pe.wait_ge(s_y, NC * at.level + jp // (CB // SJ) + 1)

            def plain(at, jp, epilogue):
                run(epilogue)
                chunk_start(at, jp)
                n = STEPS * plain_chunk(at.p, at.ic) + jp
                pe.wait_ge(s_ahi, n + 1)
                pe.wait_ge(s_alo, n + 1)
                for s in range(SJ):
                    mm = product(at, jp, s)
                mm.then_inc(s_mm, 1)

            def logit(u):
                ic, j = divmod(u, NB)
                if u >= 1:
                    pe.wait_ge(s_pr, u)
                if ic == 0 and j % CB == 0:
                    pe.wait_ge(s_qk, nth("qk", 5, j // CB, 1))
                terms = [(kT_hi, qT_hi), (kT_hi, qT_lo), (kT_lo, qT_hi)]
                for t, (k, q) in enumerate(terms):
                    for h in range(HALVES):
                        mm = pe.matmul(logits[:, h * BANK:(h + 1) * BANK], blk(k, j),
                                       q[:, ic * CH + h * BANK:ic * CH + (h + 1) * BANK], start=(t == 0), stop=(t == 2))
                mm.then_inc(s_lg, 1)

            def gated(at, jp, epilogue):
                run(epilogue)
                if at.ic == 0 and jp == 0:
                    for u in range(AHEAD):
                        logit(u)
                for s in range(SJ):
                    u = NB * at.ic + jp * SJ + s
                    if u + AHEAD < NB * NC:
                        logit(u + AHEAD)
                    if s == 0:
                        chunk_start(at, jp)
                    pe.wait_ge(s_ghi, u + 1)
                    pe.wait_ge(s_glo, u + 1)
                    product(at, jp, s).then_inc(s_gm, 1)

            pe.wait_ge(s_id, 1)
            pe.wait_ge(s_small, SMALL)
            pe.wait_ge(s_xt, 16)
            for ic in range(NC):
                if ic >= 1:
                    pe.wait_ge(s_y, ic)
                write_rows(by_node((lambda b: blk(x_T, ic * CB + b), w1[:])))
            schedule(pe, plain, gated, stages, 0, 0)

        @block.scalar
        def _(act):
            for dst, src in small:
                act.dma_start(dst, src).then_inc(s_small, 16)

            def y_slice(buf, p, ic):
                return buf[:, p % 2, bass.ds(ic * CH, CH)]

            def evacuate(ended):
                p, ic = ended.p, ended.ic
                g = NC * (p - 1) + ic
                if p == GATED:
                    act.wait_ge(s_gm, NB * (ic + 1))
                else:
                    act.wait_ge(s_mm, STEPS * (plain_chunk(p, ic) + 1))
                if p < PASSES or ic == 0:
                    act.wait_ge(s_y, NC + g)
                else:
                    act.wait_ge(s_xs, nth("xsave", p, ic) - 1)
                if p in (5, 6):
                    act.wait_ge(s_xs, nth("xsave", p, ic) - 1)
                if p in (7,):
                    act.wait_ge(s_xs, nth("xsave", GATED, NC - 1))
                scale = 2.0 ** -((G_EXP if p == GATED else A_EXP) + Y_EXP[p - 1])
                act.activation(z_T[:, :], acc[:, ended.half, :], ACT.Relu if p == 2 else ACT.Copy,
                               scale=scale).then_inc(s_zt, 1)

            def y_high(ended):
                p, ic = ended.p, ended.ic
                if p in (0, 2, 5):
                    act.wait_ge(s_rows, nth("rows", p, ic, PER_CHUNK["rows"][p] - 1))
                    src = rows_flat
                elif p in (1, 3):
                    act.wait_ge(s_val, nth("val", p, ic))
                    src = val[:, :, :].rearrange("p b f -> p (b f)")
                elif p == 7:
                    act.wait_ge(s_sw, nth("swished", p, ic))
                    src = val[:, :, :].rearrange("p b f -> p (b f)")
                else:
                    act.wait_ge(s_ln, nth("ln", p, ic, PER_CHUNK["ln"][p] - 1))
                    src = xn[:, :, :].rearrange("p b f -> p (b f)")
                act.activation(y_slice(y_hi, p, ic), src, ACT.Copy, scale=2.0 ** Y_EXP[p]).then_inc(s_yhi, 1)

            def square(k):
                def go(ended):
                    p, ic = ended.p, ended.ic
                    act.wait_ge(s_cen, nth("ln", p, ic, k))
                    act.activation(tmp[:, :, :], val[:, :, :], ACT.Square).then_inc(s_sqr, 1)
                return go

            def root(k):
                def go(ended):
                    act.wait_ge(s_var, nth("ln", ended.p, ended.ic, k))
                    act.activation(stats[:, 4, :], stats[:, 3, :], ACT.Sqrt).then_inc(s_root, 1)
                return go

            def save_x_T(ended):
                p, ic = ended.p, ended.ic
                act.wait_ge(s_rows, nth("rows", p, ic, 1))
                act.activation(x_T[:, bass.ds(ic * CH, CH)], rows_flat, ACT.Copy).then_inc(s_xT, 1)

            def save_m_T(ended):
                p, ic = ended.p, ended.ic
                act.wait_ge(s_rows, nth("rows", p, ic, 2))
                act.activation(m_T, rows_flat, ACT.Identity, bias=bmsg[:, 0:1]).then_inc(s_msg, 1)

            def qk_high(k, dst, exp):
                def go(ended):
                    p, ic = ended.p, ended.ic
                    act.wait_ge(s_rows, nth("rows", p, ic, 3 + k))
                    act.activation(dst[:, ic * CH:(ic + 1) * CH], rows_flat, ACT.Copy,
                                   scale=2.0 ** exp).then_inc(s_qkhi, 1)
                return go

            def relu(ended):
                p, ic = ended.p, ended.ic
                act.wait_ge(s_val, nth("val", p, ic))
                act.activation(val[:, :, :], val[:, :, :], ACT.Relu).then_inc(s_nl, 1)

            def sigmoid(ended):
                p, ic = ended.p, ended.ic
                act.wait_ge(s_val, nth("val", p, ic))
                act.activation(tmp[:, :, :], val[:, :, :], ACT.Sigmoid).then_inc(s_nl, 1)

            def stages(p):
                return {
                    1: {0: [evacuate], 2: [y_high]}, 3: {0: [evacuate], 2: [y_high]}, 2: {0: [evacuate], 2: [y_high]},
                    4: {0: [evacuate], 2: [square(0)], 3: [root(0)], 4: [save_x_T, y_high]},
                    5: {0: [evacuate], 2: [square(0)], 3: [root(0)], 4: [save_x_T], 5: [save_m_T], 6: [qk_high(0, qT_hi, Q_EXP)],
                        7: [qk_high(1, kT_hi, K_EXP)], 8: [y_high]},
                    6: {0: [evacuate], 2: [relu], 3: [square(0)], 4: [root(0)], 6: [square(1)], 7: [root(1)], 8: [y_high]},
                    7: {0: [evacuate], 2: [sigmoid], 3: [y_high]},
                    8: {0: [evacuate], 2: [sigmoid], 4: [square(0)], 5: [root(0)]},
                }[p]

            def plain(at, jp, epilogue):
                p, ic = at.p, at.ic
                g = NC * (p - 1) + ic
                n = STEPS * plain_chunk(p, ic) + jp
                act.wait_ge(s_a[jp % RING], 16 * ((STEPS // RING) * g + jp // RING + 1))
                if after_gated(at) and jp < RING:
                    act.wait_ge(s_gm, NB * NC - SJ * RING + SJ * (jp + 1))
                elif not (isinstance(n, int) and n < RING):
                    act.wait_ge(s_mm, n - RING + 1)
                act.activation(a_hi[:, jp % RING, :, :], a_ring[:, jp % RING, :, :], ACT.Copy,
                               scale=2.0 ** A_EXP).then_inc(s_ahi, 1)
                run(epilogue)

            def gated(at, jp, epilogue):
                p, ic = at.p, at.ic
                def gate_high(u):
                    act.wait_ge(s_g, u + 1)
                    if u < SJ * RING:
                        act.wait_ge(s_mm, STEPS * plain_chunk(GATED - 1, NC) - RING + u // SJ + 1)
                    else:
                        act.wait_ge(s_gm, u - SJ * RING + 1)
                    act.activation(a_hi[:, (u // SJ) % RING, u % SJ, :], gates[:, u % 2, :], ACT.Copy).then_inc(s_ghi, 1)

                for s in range(SJ):
                    u = NB * ic + jp * SJ + s
                    act.wait_ge(s_lg, u + 1)
                    if u >= 2:
                        act.wait_ge(s_glo, u - 1)
                    act.activation(gates[:, u % 2, :], logits[:, :], ACT.Sigmoid, bias=gbias[:, 0:1],
                                   scale=2.0 ** -(Q_EXP + K_EXP) * F ** -0.5).then_inc(s_pr, 1)
                    if u >= 1:
                        gate_high(u - 1)
                    if u == NB * NC - 1:
                        gate_high(u)
                run(epilogue)

            act.wait_ge(s_small, SMALL)
            for ic in range(NC):
                y_high(Chunk(0, ic, None, 0, 0, 0))
            schedule(act, plain, gated, stages, 3, 1)

        @block.vector
        def _(dve):
            def y_low(ended):
                p, ic = ended.p, ended.ic
                dve.wait_ge(s_yhi, nth("yhi", p, ic))
                hi = y_hi[:, p % 2, bass.ds(ic * CH, CH)]
                lo = y_lo[:, p % 2, bass.ds(ic * CH, CH)]
                if p in (0, 2, 5):
                    src = rows_flat
                elif p in (1, 3, 7):
                    src = val[:, :, :].rearrange("p b f -> p (b f)")
                else:
                    src = xn[:, :, :].rearrange("p b f -> p (b f)")
                op = dve.scalar_tensor_tensor(out=lo, in0=src, scalar=2.0 ** Y_EXP[p], in1=hi, op0=ALU.mult,
                                              op1=ALU.subtract)
                op.then_inc(s_y, 1)

            def values(ended):
                p, ic = ended.p, ended.ic
                dve.wait_ge(s_rows, nth("rows", p, ic))
                right, op = {
                    1: lambda: (over_features(f1c[:, bass.ds(ic * CB, CB)]), ALU.mult),
                    3: lambda: (over_features(f2c[:, bass.ds(ic * CB, CB)]), ALU.mult),
                    4: lambda: (x_chunk(ic), ALU.add), 5: lambda: (x_chunk(ic), ALU.add),
                    6: lambda: (over_blocks(bupd), ALU.add), 7: lambda: (over_blocks(b3r), ALU.add),
                    8: lambda: (over_blocks(b3r), ALU.add)}[p]()
                ins = dve.tensor_tensor(val[:, :, :], rows[:, :, :], right, op)
                ins.then_inc(s_val, 1)

            def swish(ended):
                p, ic = ended.p, ended.ic
                dve.wait_ge(s_nl, nth("nonlin", p, ic))
                dve.tensor_tensor(val[:, :, :], val[:, :, :], tmp[:, :, :], ALU.mult).then_inc(s_sw, 1)

            def residual(ended):
                p, ic = ended.p, ended.ic
                dve.wait_ge(s_sw, nth("swished", p, ic))
                dve.tensor_tensor(val[:, :, :], val[:, :, :], x_chunk(ic), ALU.add).then_inc(s_res, 1)

            def ln_mean(k, ready, ready_stage, kk=0):
                def go(ended):
                    p, ic = ended.p, ended.ic
                    n = nth("ln", p, ic, k)
                    dve.wait_ge(ready, nth(ready_stage, p, ic, kk))
                    dve.tensor_reduce(stats[:, 0, :], val[:, :, :], AX, ALU.add).then_inc(s_sum, 1)
                    dve.wait_ge(s_sum, n)
                    dve.tensor_scalar(stats[:, 1, :], stats[:, 0, :], 1.0 / F, None, ALU.mult).then_inc(s_mean, 1)
                return go

            def ln_var(k):
                def go(ended):
                    p, ic = ended.p, ended.ic
                    n = nth("ln", p, ic, k)
                    dve.wait_ge(s_sqr, n)
                    dve.tensor_reduce(stats[:, 2, :], tmp[:, :, :], AX, ALU.add).then_inc(s_ss, 1)
                    dve.wait_ge(s_ss, n)
                    dve.tensor_scalar(stats[:, 3, :], stats[:, 2, :], 1.0 / F, LN_EPS, ALU.mult, ALU.add).then_inc(s_var, 1)
                return go

            def ln_rstd(k):
                def go(ended):
                    n = nth("ln", ended.p, ended.ic, k)
                    dve.wait_ge(s_root, n)
                    dve.reciprocal(stats[:, 5, :], stats[:, 4, :]).then_inc(s_inv, 1)
                    dve.wait_ge(s_inv, n)
                    dve.tensor_tensor(stats[:, 6, :], stats[:, 5, :], stats[:, 5, :], ALU.mult).then_inc(s_newton, 1)
                    dve.wait_ge(s_newton, NEWTON * (n - 1) + 1)
                    dve.tensor_tensor(stats[:, 6, :], stats[:, 6, :], stats[:, 3, :], ALU.mult).then_inc(s_newton, 1)
                    dve.wait_ge(s_newton, NEWTON * (n - 1) + 2)
                    dve.tensor_scalar(stats[:, 6, :], stats[:, 6, :], -0.5, 1.5, ALU.mult, ALU.add).then_inc(s_newton, 1)
                    dve.wait_ge(s_newton, NEWTON * n)
                    dve.tensor_tensor(stats[:, 7, :], stats[:, 5, :], stats[:, 6, :], ALU.mult).then_inc(s_rstd, 1)
                return go

            def qk_low(k, hi, lo, exp):
                def go(ended):
                    p, ic = ended.p, ended.ic
                    dve.wait_ge(s_qkhi, nth("qk", p, ic, k))
                    ins = dve.scalar_tensor_tensor(out=lo[:, ic * CH:(ic + 1) * CH], in0=rows_flat, scalar=2.0 ** exp,
                                                   in1=hi[:, ic * CH:(ic + 1) * CH], op0=ALU.mult, op1=ALU.subtract)
                    ins.then_inc(s_qk, 1)
                return go

            def stages(p):
                return {
                    1: {1: [values], 2: [y_low]}, 3: {1: [values], 2: [y_low]}, 2: {2: [y_low]},
                    4: {1: [values, ln_mean(0, s_val, "val")], 2: [ln_var(0)], 3: [ln_rstd(0)], 4: [y_low]},
                    5: {1: [values, ln_mean(0, s_val, "val")], 2: [ln_var(0)], 3: [ln_rstd(0)],
                        6: [qk_low(0, qT_hi, qT_lo, Q_EXP)], 7: [qk_low(1, kT_hi, kT_lo, K_EXP)], 8: [y_low]},
                    6: {1: [values], 2: [ln_mean(0, s_nl, "nonlin")], 3: [ln_var(0)], 4: [ln_rstd(0)],
                        5: [ln_mean(1, s_aff, "affine", 2)], 6: [ln_var(1)], 7: [ln_rstd(1)], 8: [y_low]},
                    7: {1: [values], 2: [swish], 3: [y_low]},
                    8: {1: [values], 2: [swish], 3: [residual, ln_mean(0, s_res, "resid")], 4: [ln_var(0)],
                        5: [ln_rstd(0)]},
                }[p]

            def plain(at, jp, epilogue):
                p, ic = at.p, at.ic
                dve.wait_ge(s_ahi, STEPS * plain_chunk(p, ic) + jp + 1)
                dve.scalar_tensor_tensor(out=a_lo[:, jp % RING, :, :].rearrange("p s c -> p (s c)"),
                                         in0=a_ring[:, jp % RING, :, :].rearrange("p s c -> p (s c)"), scalar=2.0 ** A_EXP,
                                         in1=a_hi[:, jp % RING, :, :].rearrange("p s c -> p (s c)"), op0=ALU.mult,
                                         op1=ALU.subtract).then_inc(s_alo, 1)
                run(epilogue)

            def gated(at, jp, epilogue):
                p, ic = at.p, at.ic
                def gate_low(u):
                    dve.wait_ge(s_ghi, u + 1)
                    dve.tensor_tensor(a_lo[:, (u // SJ) % RING, u % SJ, :], gates[:, u % 2, :],
                                      a_hi[:, (u // SJ) % RING, u % SJ, :], ALU.subtract).then_inc(s_glo, 1)

                for s in range(SJ):
                    u = NB * ic + jp * SJ + s
                    dve.wait_ge(s_pr, u + 1)
                    dve.wait_ge(s_sq, u + 1)
                    dve.scalar_tensor_tensor(out=gates[:, u % 2, :], in0=gates[:, u % 2, :], scalar=2.0 ** G_EXP,
                                             in1=a_sq[:, u % 2, :], op0=ALU.mult, op1=ALU.mult).then_inc(s_g, 1)
                    if u >= 1:
                        gate_low(u - 1)
                    if u == NB * NC - 1:
                        gate_low(u)
                run(epilogue)

            dve.wait_ge(s_small, SMALL)
            for ic in range(NC):
                y_low(Chunk(0, ic, None, 0, 0, 0))
            schedule(dve, plain, gated, stages, 3, 1)

        @block.gpsimd
        def _(pool):
            pool.memset(ident[:, :], 0.0).then_inc(s_id0, 1)
            pool.wait_ge(s_id0, 1)
            pool.affine_select(out=ident[:, :], in_=ident[:, :], compare_op=ALU.not_equal, fill=1.0, base=0,
                               pattern=[[-1, P]], channel_multiplier=1).then_inc(s_id, 1)

            def centre(k):
                def go(ended):
                    p, ic = ended.p, ended.ic
                    pool.wait_ge(s_mean, nth("ln", p, ic, k))
                    pool.tensor_tensor(val[:, :, :], val[:, :, :], over_features(stats[:, 1, :]),
                                       ALU.subtract).then_inc(s_cen, 1)
                return go

            def normalise(k):
                def go(ended):
                    p, ic = ended.p, ended.ic
                    pool.wait_ge(s_rstd, nth("ln", p, ic, k))
                    pool.tensor_tensor(xn[:, :, :], val[:, :, :], over_features(stats[:, 7, :]),
                                       ALU.mult).then_inc(s_ln, 1)
                return go

            def save_x(ended):
                p, ic = ended.p, ended.ic
                pool.wait_ge(s_ln, nth("ln", p, ic, PER_CHUNK["ln"][p] - 1))
                pool.tensor_copy(x_chunk(ic), xn[:, :, :]).then_inc(s_xs, 1)

            def affine(ended):
                p, ic = ended.p, ended.ic
                pool.wait_ge(s_ln, nth("ln", p, ic, 0))
                pool.tensor_tensor(xn[:, :, :], xn[:, :, :], over_blocks(gam), ALU.mult).then_inc(s_aff, 1)
                pool.wait_ge(s_aff, nth("affine", p, ic, 0))
                pool.tensor_tensor(xn[:, :, :], xn[:, :, :], over_blocks(bet), ALU.add).then_inc(s_aff, 1)
                pool.wait_ge(s_aff, nth("affine", p, ic, 1))
                pool.tensor_tensor(val[:, :, :], xn[:, :, :], x_chunk(ic), ALU.add).then_inc(s_aff, 1)

            def stages(p):
                return {
                    4: {2: [centre(0)], 3: [normalise(0), save_x]},
                    5: {2: [centre(0)], 3: [normalise(0), save_x]},
                    6: {2: [centre(0)], 4: [normalise(0), affine], 6: [centre(1)], 7: [normalise(1), save_x]},
                    8: {3: [centre(0)], 5: [normalise(0), save_x]},
                }.get(p, {})

            def gated(at, jp, epilogue):
                p, ic = at.p, at.ic
                for s in range(SJ):
                    u = NB * ic + jp * SJ + s
                    if s == 0:
                        pool.wait_ge(s_a[jp % RING], 16 * ((STEPS // RING) * (NC * (p - 1) + ic) + jp // RING + 1))
                    if u >= 2:
                        pool.wait_ge(s_g, u - 1)
                    pool.tensor_tensor(a_sq[:, u % 2, :], a_ring[:, jp % RING, s, :], a_ring[:, jp % RING, s, :],
                                       ALU.mult).then_inc(s_sq, 1)
                run(epilogue)

            pool.wait_ge(s_small, SMALL)
            schedule(pool, None, gated, stages, 3, 1)


def kernel(**inputs):
    import numpy as np
    import concourse.bacc as bacc
    from concourse.bass_utils import run_bass_kernel_spmd

    def columns(v):
        return np.ascontiguousarray(v.reshape(NB, P).T)

    adj = np.asarray(inputs["adj"])
    x = np.asarray(inputs["x"])
    laid_out = {
        "adj": np.ascontiguousarray(adj.reshape(NC, CH, STEPS, SJ, P).transpose(0, 2, 4, 3, 1)),
        "x": np.ascontiguousarray(x.reshape(NB, P, F).transpose(1, 0, 2)),
        "xt": np.ascontiguousarray(x.T),
        "W1": np.asarray(inputs["L0_gnn_W1"]), "f1": columns(np.asarray(inputs["L0_gnn_f1"])),
        "W2": np.asarray(inputs["L0_gnn_W2"]), "f2": columns(np.asarray(inputs["L0_gnn_f2"])),
        "Wcat": np.asarray(inputs["L1_gnn_weight"]),
        "W_msg": np.asarray(inputs["L2_gnn_W_msg"]), "b_msg": np.asarray(inputs["L2_gnn_b_msg"]),
        "W_q": np.asarray(inputs["L2_gnn_W_q"]), "W_k": np.asarray(inputs["L2_gnn_W_k"]),
        "gate_bias": np.asarray(inputs["L2_gnn_gate_bias"]).reshape(1),
        "W_upd": np.asarray(inputs["L2_gnn_W_upd"]), "b_upd": np.asarray(inputs["L2_gnn_b_upd"]),
        "ln_g": np.asarray(inputs["L2_gnn_ln_gamma"]), "ln_b": np.asarray(inputs["L2_gnn_ln_beta"]),
        "W3": np.asarray(inputs["L3_gnn_W"]), "b3": np.asarray(inputs["L3_gnn_b"]),
    }
    nc = bacc.Bacc("TRN2", target_bir_lowering=False, num_devices=1)
    arrays, args = {}, {}
    for name, a in laid_out.items():
        arrays[f"{name}_dram"] = a
        args[name] = nc.dram_tensor(f"{name}_dram", a.shape, mybir.dt.from_np(a.dtype), kind="ExternalInput").ap()
    args["out"] = nc.dram_tensor("out_dram", (P, NB, F), F32, kind="ExternalOutput").ap()
    build(nc, **args)
    r = run_bass_kernel_spmd(nc, [arrays], core_ids=[0])
    return np.ascontiguousarray(r.results[0]["out_dram"].transpose(1, 0, 2)).reshape(N, F)
```

```python
from collections import namedtuple
from contextlib import ExitStack

import concourse.bass as bass
from concourse import mybir

P = 128
N = 4096
F = 128
NB = N // P
CH = 1024
NC = N // CH
CB = CH // P
SJ = 2
STEPS = NB // SJ
RING = 4
BANK = 512
HALVES = CH // BANK
PASSES = 8
GATED = 6
AHEAD = 4
LONE_LOGITS = 6
ACT_SQUARES = 8

A_EXP = 10
G_EXP = 12
Y_EXP = [3, -2, 0, -5, 5, 2, 5, 5]
Q_EXP, K_EXP = -3, 4
LN_EPS = 1e-5
RSQRT_GUESS = 0x5F3759DF
G_RING = 4
NEWTON = 3

ALU = mybir.AluOpType
ACT = mybir.ActivationFunctionType
AX = mybir.AxisListType.X
F32 = mybir.dt.float32
F16 = mybir.dt.float16

UP, DOWN = [0, 1, 2, 3], [3, 2, 1, 0]
ORDER = {0: UP, 1: UP, 2: DOWN, 3: UP, 4: DOWN, 5: UP, 6: UP, 7: UP, 8: DOWN}
WHOLE = (1, 7)
HALF = (2, 3, 4, 5, 8)
AHEAD_OF = (1, 2, 3, 4, 7)
LATE = (4,)

PER_CHUNK = {
    "rows": {0: 1, 1: 1, 2: 1, 3: 1, 4: 2, 5: 5, 6: 1, 7: 2, 8: 2},
    "x_T": {4: 1, 5: 1},
    "relu_z": {2: 1},
    "val": {1: 1, 3: 1, 4: 1, 5: 1, 6: 1},
    "nonlin": {6: 1, 7: 1, 8: 1},
    "swished": {7: 1, 8: 1},
    "resid": {6: 1, 8: 1},
    "affine": {6: 2},
    "ln": {4: 1, 5: 1, 6: 2, 8: 1},
    "msg": {5: 1},
    "qk": {5: 2},
}


def nth(stage, p, k, run=0):
    per = PER_CHUNK[stage]
    return NC * sum(n for q, n in per.items() if q < p) + per[p] * k + run + 1


OWN, BOTH, TAIL = "own", "own and next, step by step", "own, then next"
GROUP = STEPS // NC
Block = namedtuple("Block", "p k i j mode")


def blocks_of(p):
    o = ORDER[p]
    both, last = (BOTH, TAIL) if p in AHEAD_OF else (OWN, OWN)
    if p == GATED:
        at = [(k, j, OWN) for k in range(NC) for j in range(NC)]
    elif p in WHOLE:
        at = [(0, 0, OWN), (0, 1, OWN), (0, 2, OWN), (1, 1, OWN), (0, 3, OWN), (1, 2, OWN), (1, 3, OWN), (1, 0, both),
              (2, 2, OWN), (2, 3, OWN), (2, 0, both), (2, 1, both), (3, 3, OWN), (3, 0, both), (3, 1, both),
              (3, 2, last)]
    else:
        at = [(1, 1, OWN), (0, 0, OWN), (1, 0, OWN if p in LATE else last), (2, 2, OWN), (2, 0, both), (2, 1, both),
              (3, 3, OWN), (3, 0, both), (3, 1, both), (3, 2, last)]
        if p - 1 in LATE:
            at.insert(3, (2, 3, OWN))
    return [Block(p, k, o[k], o[j], mode) for k, j, mode in at]


Step = namedtuple("Step", "n p k i j0")
Unit = namedtuple("Unit", "step use s first last")


def plan():
    steps, units = [], []
    for p in range(1, PASSES + 1):
        for b in blocks_of(p):
            group = [Step(len(steps) + t, p, b.k, b.i, (b.j * GROUP + t) * SJ) for t in range(GROUP)]
            steps += group
            if p == GATED:
                units += [(st, "own", s) for st in group for s in range(SJ)]
            elif b.mode == BOTH:
                units += [(st, use, None) for st in group for use in ("own", "next")]
            else:
                units += [(st, "own", None) for st in group]
                if b.mode == TAIL:
                    units += [(st, "next", None) for st in group]
    key = [(st.p, st.k, use) for st, use, _ in units]
    first, last = {}, {}
    for n, x in enumerate(key):
        first.setdefault(x, n)
        last[x] = n
    return steps, [Unit(st, use, s, first[x] == n, last[x] == n) for n, ((st, use, s), x) in enumerate(zip(units, key))]


STREAM, UNITS = plan()
FIRST_USE, LAST_USE, SUM_DONE = {}, {}, {}
for _n, _u in enumerate(UNITS):
    FIRST_USE.setdefault(_u.step.n, _n)
    LAST_USE[_u.step.n] = _n
    SUM_DONE[_u.step.p, _u.step.k, _u.use] = _n
PLAIN_BEFORE = [sum(st.p != GATED for st in STREAM[:n]) for n in range(len(STREAM) + 1)]
GATED_FROM = PLAIN_BEFORE.index(PLAIN_BEFORE[-1] - sum(st.p > GATED for st in STREAM))
SAVED = sorted((p, k) for p, k, use in SUM_DONE if use == "next")

LENGTH = {0: 1, 1: 3, 2: 3, 3: 3, 4: 6, 5: 10, 6: 15, 7: 4, 8: 9}


def epilogues():
    out = [(0, k, k) for k in range(NC)]
    for p in range(1, PASSES + 1):
        for k in range(NC):
            q, _, before = out[-1]
            out.append((p, k, max(SUM_DONE[p, k, "own"] + 1, before + LENGTH[q])))
    return out


EPILOGUES = epilogues()


def epilogue_by_unit():
    at = {}
    for p, k in SAVED:
        at.setdefault(SUM_DONE[p, k, "next"] + 1, []).append((p, k, "save"))
    for p, k, start in EPILOGUES:
        for t in range(LENGTH[p] + 1):
            at.setdefault(start + t, []).append((p, k, t))
    return at


DUE_AT = epilogue_by_unit()
THE_END = max(DUE_AT)


def build(nc, adj, x, xt, W1, f1, W2, f2, Wcat, W_msg, b_msg, W_qT, W_kT, gate_bias, W_upd, b_upd, ln_g, ln_b, W3, b3, out):
    with ExitStack() as ctx:
        def sb(name, shape, dt=F32):
            return ctx.enter_context(nc.sbuf_tensor(name, shape, dt))

        def sem(name):
            return ctx.enter_context(nc.semaphore(name))

        a_ring = sb("a_ring", [P, RING, SJ, CH])
        a_hi = sb("a_hi", [P, RING, SJ, CH], F16)
        a_lo = sb("a_lo", [P, RING, SJ, CH], F16)
        y_hi = sb("y_hi", [P, 2, N], F16)
        y_lo = sb("y_lo", [P, 2, N], F16)
        x_rows = sb("x_rows", [P, NB, F])
        x_T = sb("x_T", [P, N])
        qT_hi, qT_lo = sb("qT_hi", [P, N], F16), sb("qT_lo", [P, N], F16)
        kT_hi, kT_lo = sb("kT_hi", [P, N], F16), sb("kT_lo", [P, N], F16)
        gates = sb("gates", [P, G_RING, CH])
        z_T = sb("z_T", [P, CH])
        val = sb("val", [P, CB, F])
        tmp = sb("tmp", [P, CB, F])
        tmp_T = tmp[:, :, :].rearrange("p b f -> p (b f)")
        xn = sb("xn", [P, CB, F])
        xn_T = xn[:, :, :].rearrange("p b f -> p (b f)")
        bn = sb("bn", [P, CB, 6])
        moments = sb("moments", [P, CB, 2])
        stats = sb("stats", [P, 3, CB])
        ident = sb("ident", [P, P])
        w1, w2, w3 = sb("w1", [P, F]), sb("w2", [P, F]), sb("w3", [P, F])
        wcat, wupd = sb("wcat", [P, 2, F]), sb("wupd", [P, 2, F])
        wmsg, wqT, wkT, w_qk = sb("wmsg", [P, F]), sb("wqT", [P, F]), sb("wkT", [P, F]), sb("w_qk", [P, F])
        f1c, f2c = sb("f1c", [P, NB]), sb("f2c", [P, NB])
        bmsg, gbias, b3c = sb("bmsg", [P, 1]), sb("gbias", [P, 1]), sb("b3c", [P, 1])
        bupd, gam, bet = sb("bupd", [P, F]), sb("gam", [P, F]), sb("bet", [P, F])

        acc = ctx.enter_context(nc.psum_tensor("acc", [P, 2, CH], F32))
        spare = ctx.enter_context(nc.psum_tensor("spare", [P, CH], F32))
        rows = ctx.enter_context(nc.psum_tensor("rows", [P, CB, F], F32))

        s_small = sem("small_loaded")
        s_w1, s_x = sem("w1_loaded"), sem("x_loaded")
        s_xt = [sem(f"xt_loaded{i}") for i in range(NC)]
        s_a = [sem(f"a_loaded{i}") for i in range(RING)]
        s_id0, s_id = sem("ident_zero"), sem("ident_ready")
        s_ahi, s_alo, s_unit = sem("a_hi_ready"), sem("a_lo_ready"), sem("unit_multiplied")
        s_lg, s_pr = sem("logits_ready"), sem("probs_ready")
        s_sq, s_sqa = sem("squares_by_gpsimd"), sem("squares_by_scalar")
        s_g, s_ghi, s_glo = sem("gates_ready"), sem("g_hi_ready"), sem("g_lo_ready")
        s_rows, s_xT = sem("rows_written"), sem("x_T_saved")
        s_zt, s_val, s_nl, s_sw = sem("z_T_ready"), sem("val_ready"), sem("nonlinearity_done"), sem("swish_done")
        s_res, s_aff = sem("residual_added"), sem("affine_done")
        s_bn, s_moments, s_cen, s_var, s_ln = sem("ln_bn"), sem("ln_moments"), sem("ln_centred"), sem("ln_var"), sem("ln_done")
        s_guess, s_newton = sem("ln_guess"), sem("ln_newton")
        s_yhi, s_y = sem("y_hi_ready"), sem("y_ready")
        s_saved, s_zrelu = sem("next_sums_saved"), sem("z_T_relu_done")
        s_wqk_product, s_wqk = sem("w_qk_product"), sem("w_qk_ready")
        s_msg, s_qkhi, s_qk = sem("m_T_ready"), sem("qk_hi_ready"), sem("qk_ready")
        s_out = sem("out_stored")

        small = [(w2[:], W2), (w3[:], W3), (wmsg[:], W_msg), (wqT[:], W_qT),
                 (wkT[:], W_kT), (wcat[:, :, :], Wcat.rearrange("(t k) n -> k t n", t=2)),
                 (wupd[:, :, :], W_upd.rearrange("(t k) n -> k t n", t=2)), (f1c[:], f1), (f2c[:], f2),
                 (bmsg[:], b_msg.rearrange("(k a) -> k a", a=1)), (gbias[:], gate_bias.partition_broadcast(P)),
                 (bupd[:], b_upd.partition_broadcast(P)), (gam[:], ln_g.partition_broadcast(P)),
                 (bet[:], ln_b.partition_broadcast(P)), (b3c[:], b3.rearrange("(k a) -> k a", a=1))]
        SMALL = 16 * len(small)

        def blk(t, b):
            return t[:, b * P:(b + 1) * P]

        def over_blocks(v):
            return v[:, :].unsqueeze(1).to_broadcast([P, CB, F])

        def over_features(v):
            return v.unsqueeze(2).to_broadcast([P, CB, F])

        def normalised(p, k, run=0):
            return xn[:, :, :] if p == GATED and run == 0 else x_chunk(p, k)

        def x_chunk(p, k):
            i = ORDER[p][k]
            return x_rows[:, i * CB:(i + 1) * CB, :]

        def x_T_chunk(p, k):
            i = ORDER[p][k]
            return x_T[:, i * CH:(i + 1) * CH]

        def y_chunk(y, p, k):
            i = ORDER[p][k]
            return y[:, p % 2, i * CH:(i + 1) * CH]

        def flat(v):
            return v.rearrange("p b f -> p (b f)")

        def y_ready(p, j):
            return NC * p + ORDER[p].index(j) + 1

        def epilogue(stages, since, until):
            for n in range(since, until + 1):
                for p, k, t in DUE_AT.get(n, []):
                    for stage in stages[p].get(t, []) if p in stages else []:
                        stage(p, k)
            return max(since, until + 1)

        def freed(st):
            return LAST_USE[st.n - RING] + 1 if st.n >= RING else 0

        def slot(t, st):
            return t[:, st.n % RING, :, :]

        def part(i):
            return gates[:, i, :]

        def gated_index(st, s):
            return (st.n - GATED_FROM) * SJ + s

        def in_idle_sums(u):
            return u % NB >= LONE_LOGITS and (u - LONE_LOGITS) % 2 == 0

        def logits_of(u):
            return acc[:, (u // NB + 1) % 2, :] if in_idle_sums(u) else spare[:, :]

        def logits_before(u):
            v = u - 1
            while v >= 0 and in_idle_sums(v) != in_idle_sums(u):
                v -= 1
            return v if in_idle_sums(u) is False or v // NB == u // NB else -1

        def takes_over(p, k):
            return (p - 1, NC - 1 - k) in SAVED

        def back(p):
            return 2.0 ** -((G_EXP if p == GATED else A_EXP) + Y_EXP[p - 1])

        def buffers_free(eng, p, k):
            if p == PASSES and k:
                eng.wait_ge(s_ln, nth("ln", p, k - 1))
            else:
                eng.wait_ge(s_y, NC * p + k)
            if p in (4, 5) and (p, k) != (4, 0):
                q, kk = (p, k - 1) if k else (p - 1, NC - 1)
                eng.wait_ge(s_xT, nth("x_T", q, kk))

        def y_source(p, k):
            if p in (0, 2, 5, 7):
                return flat(rows[:, :, :])
            return flat(val[:, :, :]) if p in (1, 3) else flat(normalised(p, k, 1))

        block = ctx.enter_context(nc.Block())

        @block.sync
        def _(sp):
            def load(st):
                if st.n >= RING:
                    before = STREAM[st.n - RING]
                    if before.p == GATED:
                        sp.wait_ge(s_g, gated_index(before, SJ - 1) + 1)
                    else:
                        sp.wait_ge(s_alo, PLAIN_BEFORE[before.n] + 1)
                sp.dma_start(slot(a_ring, st), adj[st.i, st.j0 // SJ]).then_inc(s_a[st.n % RING], 16)

            for ic in range(NC):
                sp.dma_start(x_T[:, ic * CH:(ic + 1) * CH], xt[:, ic * CH:(ic + 1) * CH]).then_inc(s_xt[ic], 16)
                load(STREAM[ic])
            for st in STREAM[NC:]:
                load(st)
            sp.wait_ge(s_out, 16 * NC)

        @block.tensor
        def _(pe):
            def transposes(source):
                for b in range(CB):
                    last = pe.transpose(rows[:, b, :], source(b), ident[:, :])
                last.then_inc(s_rows, 1)

            def by_node(*terms):
                for b in range(CB):
                    for t, (left, right) in enumerate(terms):
                        last = pe.matmul(rows[:, b, :], blk(left, b), right, start=(t == 0), stop=(t == len(terms) - 1))
                last.then_inc(s_rows, 1)

            def by_feature(weight, right):
                for h in range(HALVES):
                    last = pe.matmul(flat(rows[:, :, :])[:, h * BANK:(h + 1) * BANK], weight,
                                     right[:, h * BANK:(h + 1) * BANK], start=True, stop=True)
                last.then_inc(s_rows, 1)

            def project(p, k):
                if p == 0:
                    pe.wait_ge(s_xt[k], 16)
                    if k:
                        pe.wait_ge(s_y, k)
                elif p == 2:
                    pe.wait_ge(s_zrelu, nth("relu_z", p, k))
                else:
                    pe.wait_ge(s_zt, NC * (p - 1) + k + 1)
                if p == 1 and k == 0:
                    pe.wait_ge(s_id, 1)
                    pe.wait_ge(s_small, SMALL)
                if p in (1, 3, 4):
                    transposes(lambda b: blk(z_T, b))
                elif p == 5:
                    by_node((x_T_chunk(p, k), wcat[:, 0, :]), (z_T, wcat[:, 1, :]))
                elif p == 6:
                    by_node((x_T_chunk(p, k), wupd[:, 0, :]), (z_T, wupd[:, 1, :]))
                elif p == 0:
                    by_node((x_T_chunk(p, k), w1[:, :]))
                elif p == 2:
                    by_node((z_T, w2[:, :]))
                else:
                    by_feature(w3[:], z_T)

            def swished_rows(p, k):
                pe.wait_ge(s_sw, nth("swished", p, k))
                transposes(lambda b: blk(xn_T, b))

            def x_transposes(p, k):
                pe.wait_ge(s_ln, nth("ln", p, k))
                transposes(lambda b: normalised(p, k)[:, b, :])

            def messages(p, k):
                pe.wait_ge(s_xT, nth("x_T", p, k))
                by_feature(wmsg[:], x_T_chunk(p, k))

            def query_key_weights(p, k):
                if k == 0:
                    pe.wait_ge(s_small, SMALL)
                    pe.matmul(spare[:, :F], wqT[:], wkT[:], start=True, stop=True).then_inc(s_wqk_product, 1)

            def queries(p, k):
                pe.wait_ge(s_msg, nth("msg", p, k))
                by_feature(w_qk[:], tmp_T)

            def message_rows(p, k):
                pe.wait_ge(s_qk, nth("qk", p, k, 1))
                transposes(lambda b: blk(tmp_T, b))

            first = {p: {2 if p == GATED else 1: [project] + [query_key_weights] * (p == 1)} for p in range(1, PASSES + 1)}
            stages = {**first, 0: {0: [project]}, 4: {1: [project], 6: [x_transposes]},
                          5: {1: [project], 5: [x_transposes], 6: [messages], 7: [queries],
                              9: [message_rows]},
                      7: {1: [project], 3: [swished_rows]}, 8: {1: [project], 3: [swished_rows]}}
            at = 0

            def product(unit, s):
                st = unit.step
                y_pass = st.p - 1 if unit.use == "own" else st.p
                sums = acc[:, st.k % 2, :] if unit.use == "own" else spare[:, :]
                j = st.j0 + s
                begins = unit.first and s == (unit.s or 0)
                ends = unit.last and s == SJ - 1
                for t, (y, a) in enumerate([(y_hi, a_hi), (y_hi, a_lo), (y_lo, a_hi)]):
                    for h in range(HALVES):
                        mm = pe.matmul(sums[:, h * BANK:(h + 1) * BANK], blk(y[:, y_pass % 2, :], j),
                                       slot(a, st)[:, s, h * BANK:(h + 1) * BANK],
                                       start=(begins and t == 0), stop=(ends and t == 2))
                return mm

            def logit(u):
                st = STREAM[GATED_FROM + u // SJ]
                j = st.j0 + u % SJ
                before = logits_before(u)
                if before >= 0:
                    pe.wait_ge(s_pr, before + 1)
                if u % NB == LONE_LOGITS:
                    pe.wait_ge(s_zt, NC * (GATED - 1) + st.k)
                if j % CB == 0 and st.k == 0:
                    pe.wait_ge(s_qk, nth("qk", 5, ORDER[5].index(j // CB), 1 if u == 0 else 0))
                if j % CB == 0 and st.j0 // CB == ORDER[GATED][0] and st.k:
                    pe.wait_ge(s_qk, nth("qk", 5, ORDER[5].index(st.i), 1))
                for t, (k, q) in enumerate([(kT_hi, qT_hi), (kT_hi, qT_lo), (kT_lo, qT_hi)]):
                    for h in range(HALVES):
                        mm = pe.matmul(logits_of(u)[:, h * BANK:(h + 1) * BANK], blk(k, j),
                                       q[:, st.i * CH + h * BANK:st.i * CH + (h + 1) * BANK],
                                       start=(t == 0), stop=(t == 2))
                mm.then_inc(s_lg, 1)

            pe.wait_ge(s_w1, 16)
            for n, unit in enumerate(UNITS):
                at = epilogue(stages, at, n)
                if 0 <= n - FIRST_USE[GATED_FROM] + AHEAD < NB * NC:
                    logit(n - FIRST_USE[GATED_FROM] + AHEAD)
                st = unit.step
                if st.p == GATED:
                    u = gated_index(st, unit.s)
                    pe.wait_ge(s_glo, u + 1)
                elif FIRST_USE[st.n] == n:
                    pe.wait_ge(s_alo, PLAIN_BEFORE[st.n] + 1)
                if unit.first and unit.use == "own" and (st.p, st.k) not in ((1, 0), (1, 1)):
                    pe.wait_ge(s_zt, NC * (st.p - 1) + st.k - 1)
                if unit.first and unit.use == "next" and not SAVED.index((st.p, st.k)):
                    pe.wait_ge(s_wqk, 1)
                if unit.first and unit.use == "next" and SAVED.index((st.p, st.k)):
                    pe.wait_ge(s_saved, SAVED.index((st.p, st.k)))
                if st.j0 % CB == 0 and not unit.s:
                    pe.wait_ge(s_y, y_ready(st.p - 1 if unit.use == "own" else st.p, st.j0 // CB))
                for s in range(SJ) if unit.s is None else [unit.s]:
                    mm = product(unit, s)
                mm.then_inc(s_unit, 1)
            epilogue(stages, at, THE_END)

        @block.scalar
        def _(act):
            act.dma_start(w1[:], W1).then_inc(s_w1, 16)

            def evacuate(p, k):
                if not takes_over(p, k):
                    act.wait_ge(s_unit, SUM_DONE[p, k, "own"] + 1)
                    buffers_free(act, p, k)
                    act.activation(z_T[:, :], acc[:, k % 2, :], ACT.Copy, scale=back(p)).then_inc(s_zt, 1)

            def save_sums(p, k):
                i = ORDER[p][k]
                act.wait_ge(s_unit, SUM_DONE[p, k, "next"] + 1)
                act.wait_ge(s_zt, NC * (p - 1) + k + 1)
                act.activation(part(i), spare[:, :], ACT.Copy, scale=back(p + 1)).then_inc(s_saved, 1)

            def relu_z(p, k):
                act.wait_ge(s_zt, NC * (p - 1) + k + 1)
                act.activation(z_T[:, :], z_T[:, :], ACT.Relu).then_inc(s_zrelu, 1)

            def y_high(p, k):
                if p in (0, 2, 5, 7):
                    act.wait_ge(s_rows, nth("rows", p, k, PER_CHUNK["rows"][p] - 1))
                elif p in (1, 3):
                    act.wait_ge(s_val, nth("val", p, k))
                else:
                    act.wait_ge(s_ln, nth("ln", p, k, PER_CHUNK["ln"][p] - 1))
                act.activation(y_chunk(y_hi, p, k), y_source(p, k), ACT.Copy, scale=2.0 ** Y_EXP[p]).then_inc(s_yhi, 1)

            def save_x_T(p, k):
                act.wait_ge(s_rows, nth("rows", p, k, 1))
                act.activation(x_T_chunk(p, k), flat(rows[:, :, :]), ACT.Copy).then_inc(s_xT, 1)

            def save_m_T(p, k):
                act.wait_ge(s_rows, nth("rows", p, k, 2))
                act.activation(tmp_T, flat(rows[:, :, :]), ACT.Identity, bias=bmsg[:, 0:1]).then_inc(s_msg, 1)

            def save_w_qk(p, k):
                if k == 0:
                    act.wait_ge(s_wqk_product, 1)
                    act.activation(w_qk[:], spare[:, :F], ACT.Copy).then_inc(s_wqk, 1)

            def qk_high(run, dst, exp):
                def go(p, k):
                    i = ORDER[p][k]
                    if run:
                        act.wait_ge(s_rows, nth("rows", p, k, 3))
                    else:
                        act.wait_ge(s_msg, nth("msg", p, k))
                    act.activation(dst[:, i * CH:(i + 1) * CH], flat(rows[:, :, :]) if run else tmp_T, ACT.Copy,
                                   scale=2.0 ** exp).then_inc(s_qkhi, 1)
                return go

            def relu(p, k):
                act.wait_ge(s_val, nth("val", p, k))
                act.activation(val[:, :, :], val[:, :, :], ACT.Relu).then_inc(s_nl, 1)

            def sigmoid(p, k):
                act.wait_ge(s_rows, nth("rows", p, k))
                act.activation(tmp_T, flat(rows[:, :, :]), ACT.Sigmoid, bias=b3c[:, 0:1]).then_inc(s_nl, 1)

            stages = {
                0: {0: [y_high]},
                1: {0: [evacuate], 1: [save_w_qk], 2: [y_high]},
                2: {0: [evacuate, relu_z], 2: [y_high]},
                3: {0: [evacuate], 2: [y_high]},
                4: {0: [evacuate], 5: [y_high], 6: [save_x_T]},
                5: {0: [evacuate], 5: [save_x_T], 6: [save_m_T], 7: [qk_high(0, kT_hi, K_EXP)],
                    8: [qk_high(1, qT_hi, Q_EXP)], 9: [y_high]},
                6: {0: [evacuate], 4: [relu], 15: [y_high]},
                7: {0: [evacuate], 2: [sigmoid], 3: [y_high]},
                8: {0: [evacuate], 2: [sigmoid]},
            }
            for p in AHEAD_OF:
                stages[p]["save"] = [save_sums]
            at = 0

            def split_high(st):
                act.wait_ge(s_a[st.n % RING], 16 * (st.n // RING + 1))
                if st.n >= RING:
                    act.wait_ge(s_unit, freed(st))
                act.activation(slot(a_hi, st), slot(a_ring, st), ACT.Copy, scale=2.0 ** A_EXP).then_inc(s_ahi, 1)

            def gate_high(u):
                st = STREAM[GATED_FROM + u // SJ]
                act.wait_ge(s_g, u + 1)
                before = STREAM[st.n - RING]
                act.wait_ge(s_unit, LAST_USE[before.n] + 1 - (SJ - 1 - u % SJ if before.p == GATED else 0))
                act.activation(slot(a_hi, st)[:, u % SJ, :], gates[:, u % G_RING, :], ACT.Copy).then_inc(s_ghi, 1)

            for st in STREAM:
                if st.p != GATED:
                    at = epilogue(stages, at, freed(st))
                    split_high(st)
                    continue
                for s in range(SJ):
                    u = gated_index(st, s)
                    at = epilogue(stages, at, FIRST_USE[st.n] + s - AHEAD + 1)
                    if u % ACT_SQUARES == ACT_SQUARES - 1:
                        act.wait_ge(s_a[st.n % RING], 16 * (st.n // RING + 1))
                        act.activation(slot(a_ring, st)[:, s, :], slot(a_ring, st)[:, s, :], ACT.Square).then_inc(s_sqa, 1)
                    act.wait_ge(s_lg, u + 1)
                    if u >= G_RING:
                        act.wait_ge(s_glo, u - G_RING + 1)
                    elif u == 0:
                        act.wait_ge(s_zt, NC * (GATED - 1) - 1)
                    act.activation(gates[:, u % G_RING, :], logits_of(u), ACT.Sigmoid, bias=gbias[:, 0:1],
                                   scale=2.0 ** -(Q_EXP + K_EXP) * F ** -0.5).then_inc(s_pr, 1)
                    if u >= 1:
                        gate_high(u - 1)
                    if u == NB * NC - 1:
                        gate_high(u)
            epilogue(stages, at, THE_END)

        @block.vector
        def _(dve):
            def take_over(p, k):
                if takes_over(p, k):
                    i = ORDER[p][k]
                    dve.wait_ge(s_unit, SUM_DONE[p, k, "own"] + 1)
                    buffers_free(dve, p, k)
                    dve.wait_ge(s_saved, SAVED.index((p - 1, ORDER[p - 1].index(i))) + 1)
                    dve.scalar_tensor_tensor(out=z_T[:, :], in0=acc[:, k % 2, :], scalar=back(p), in1=part(i),
                                             op0=ALU.mult, op1=ALU.add).then_inc(s_zt, 1)

            def y_low(p, k):
                dve.wait_ge(s_yhi, NC * p + k + 1)
                dve.scalar_tensor_tensor(out=y_chunk(y_lo, p, k), in0=y_source(p, k), scalar=2.0 ** Y_EXP[p],
                                         in1=y_chunk(y_hi, p, k), op0=ALU.mult, op1=ALU.subtract).then_inc(s_y, 1)

            def values(p, k):
                i = ORDER[p][k]
                dve.wait_ge(s_rows, nth("rows", p, k))
                if p == 1 and k == 0:
                    dve.wait_ge(s_small, SMALL)
                if p == 4 and k == 0:
                    dve.wait_ge(s_x, 16)
                if p in (1, 3):
                    right, op = over_features((f1c if p == 1 else f2c)[:, i * CB:(i + 1) * CB]), ALU.mult
                elif p in (4, 5):
                    right, op = x_chunk(p, k), ALU.add
                else:
                    right, op = over_blocks(bupd), ALU.add
                dve.tensor_tensor(val[:, :, :], rows[:, :, :], right, op).then_inc(s_val, 1)

            def swish(p, k):
                dve.wait_ge(s_nl, nth("nonlin", p, k))
                dve.scalar_tensor_tensor(out=xn_T, in0=flat(rows[:, :, :]), scalar=b3c[:, 0:1], in1=tmp_T, op0=ALU.add,
                                         op1=ALU.mult).then_inc(s_sw, 1)

            def residual(p, k):
                if p == GATED:
                    dve.wait_ge(s_aff, nth("affine", p, k, 1))
                else:
                    dve.wait_ge(s_rows, nth("rows", p, k, 1))
                update = xn if p == GATED else rows
                dve.tensor_tensor(val[:, :, :], update[:, :, :], x_chunk(p, k), ALU.add).then_inc(s_res, 1)

            def ln_moments(run, ready, stage):
                def go(p, k):
                    dve.wait_ge(ready, nth(stage, p, k))
                    for b in range(CB):
                        dve.bn_stats(bn[:, b, :], val[:, b, :]).then_inc(s_bn, 1)
                    dve.wait_ge(s_bn, CB * nth("ln", p, k, run))
                    for b in range(CB):
                        dve.bn_aggr(moments[:, b, :], bn[:, b, :]).then_inc(s_moments, 1)
                return go

            def ln_rstd(run):
                def go(p, k):
                    n = nth("ln", p, k, run)
                    var, r, t = stats[:, 0, :], stats[:, 1, :], stats[:, 2, :]
                    as_int = lambda v: v.bitcast(mybir.dt.int32)
                    dve.wait_ge(s_moments, CB * n)
                    dve.tensor_scalar(var, moments[:, :, 1], LN_EPS, None, ALU.add).then_inc(s_var, 1)
                    dve.wait_ge(s_var, n)
                    dve.tensor_scalar(as_int(t), as_int(var), 1, None, ALU.logical_shift_right).then_inc(s_guess, 1)
                    dve.wait_ge(s_guess, 2 * n - 1)
                    dve.tensor_scalar(as_int(r), as_int(t), -1.0, float(RSQRT_GUESS), ALU.mult, ALU.add).then_inc(s_guess, 1)
                    dve.wait_ge(s_guess, 2 * n)
                    for step in range(NEWTON):
                        done = 3 * (NEWTON * (n - 1) + step)
                        if step:
                            dve.wait_ge(s_newton, done)
                        dve.tensor_tensor(t, r, r, ALU.mult).then_inc(s_newton, 1)
                        dve.wait_ge(s_newton, done + 1)
                        dve.scalar_tensor_tensor(out=t, in0=t, scalar=-0.5, in1=var, op0=ALU.mult,
                                                 op1=ALU.mult).then_inc(s_newton, 1)
                        dve.wait_ge(s_newton, done + 2)
                        dve.scalar_tensor_tensor(out=r, in0=t, scalar=1.5, in1=r, op0=ALU.add,
                                                 op1=ALU.mult).then_inc(s_newton, 1)
                return go

            def qk_low(run, hi, lo, exp):
                def go(p, k):
                    i = ORDER[p][k]
                    dve.wait_ge(s_qkhi, nth("qk", p, k, run))
                    dve.scalar_tensor_tensor(out=lo[:, i * CH:(i + 1) * CH], in0=flat(rows[:, :, :]) if run else tmp_T, scalar=2.0 ** exp,
                                             in1=hi[:, i * CH:(i + 1) * CH], op0=ALU.mult,
                                             op1=ALU.subtract).then_inc(s_qk, 1)
                return go

            stages = {
                0: {0: [y_low]},
                1: {0: [take_over], 1: [values], 2: [y_low]},
                2: {0: [take_over], 2: [y_low]},
                3: {0: [take_over], 1: [values], 2: [y_low]},
                4: {0: [take_over], 1: [values], 2: [ln_moments(0, s_val, "val"), ln_rstd(0)], 5: [y_low]},
                5: {0: [take_over], 1: [values], 2: [ln_moments(0, s_val, "val"), ln_rstd(0)],
                    7: [qk_low(0, kT_hi, kT_lo, K_EXP)], 8: [qk_low(1, qT_hi, qT_lo, Q_EXP)], 9: [y_low]},
                6: {3: [values], 5: [ln_moments(0, s_nl, "nonlin")], 6: [ln_rstd(0)],
                    9: [residual], 11: [ln_moments(1, s_res, "resid")], 12: [ln_rstd(1)], 15: [y_low]},
                7: {2: [swish], 3: [y_low]},
                8: {0: [take_over], 2: [swish], 4: [residual], 5: [ln_moments(0, s_res, "resid")], 6: [ln_rstd(0)]},
            }
            at = 0

            def split_low(st):
                dve.wait_ge(s_ahi, PLAIN_BEFORE[st.n] + 1)
                dve.scalar_tensor_tensor(out=slot(a_lo, st).rearrange("p s c -> p (s c)"),
                                         in0=slot(a_ring, st).rearrange("p s c -> p (s c)"), scalar=2.0 ** A_EXP,
                                         in1=slot(a_hi, st).rearrange("p s c -> p (s c)"), op0=ALU.mult,
                                         op1=ALU.subtract).then_inc(s_alo, 1)

            def gate_low(u):
                st = STREAM[GATED_FROM + u // SJ]
                dve.wait_ge(s_ghi, u + 1)
                dve.tensor_tensor(slot(a_lo, st)[:, u % SJ, :], gates[:, u % G_RING, :], slot(a_hi, st)[:, u % SJ, :],
                                  ALU.subtract).then_inc(s_glo, 1)

            for st in STREAM:
                if st.p != GATED:
                    at = epilogue(stages, at, freed(st))
                    split_low(st)
                    continue
                for s in range(SJ):
                    u = gated_index(st, s)
                    at = epilogue(stages, at, FIRST_USE[st.n] + s - AHEAD + 1)
                    dve.wait_ge(s_pr, u + 1)
                    if u % ACT_SQUARES == ACT_SQUARES - 1:
                        dve.wait_ge(s_sqa, u // ACT_SQUARES + 1)
                    else:
                        dve.wait_ge(s_sq, u + 1 - u // ACT_SQUARES)
                    dve.scalar_tensor_tensor(out=gates[:, u % G_RING, :], in0=gates[:, u % G_RING, :],
                                             scalar=2.0 ** G_EXP, in1=slot(a_ring, st)[:, s, :], op0=ALU.mult,
                                             op1=ALU.mult).then_inc(s_g, 1)
                    if u >= 1:
                        gate_low(u - 1)
                    if u == NB * NC - 1:
                        gate_low(u)
            epilogue(stages, at, THE_END)

        @block.gpsimd
        def _(pool):
            pool.memset(ident[:, :], 0.0).then_inc(s_id0, 1)
            pool.wait_ge(s_id0, 1)
            pool.affine_select(out=ident[:, :], in_=ident[:, :], compare_op=ALU.not_equal, fill=1.0, base=0,
                               pattern=[[-1, P]], channel_multiplier=1).then_inc(s_id, 1)

            def centre(run):
                def go(p, k):
                    pool.wait_ge(s_moments, CB * nth("ln", p, k, run))
                    pool.tensor_tensor(val[:, :, :], val[:, :, :], over_features(moments[:, :, 0]),
                                       ALU.subtract).then_inc(s_cen, 1)
                return go

            def normalise(run):
                def go(p, k):
                    n = nth("ln", p, k, run)
                    pool.wait_ge(s_cen, n)
                    pool.wait_ge(s_newton, 3 * NEWTON * n)
                    pool.tensor_tensor(normalised(p, k, run), val[:, :, :], over_features(stats[:, 1, :]),
                                       ALU.mult).then_inc(s_ln, 1)
                return go

            def store(p, k):
                i = ORDER[p][k]
                pool.wait_ge(s_ln, nth("ln", p, k))
                pool.dma_start(out[:, i * CB:(i + 1) * CB, :], x_chunk(p, k)).then_inc(s_out, 16)

            def affine(p, k):
                pool.wait_ge(s_ln, nth("ln", p, k, 0))
                pool.tensor_tensor(xn[:, :, :], xn[:, :, :], over_blocks(gam), ALU.mult).then_inc(s_aff, 1)
                pool.wait_ge(s_aff, nth("affine", p, k, 0))
                pool.tensor_tensor(xn[:, :, :], xn[:, :, :], over_blocks(bet), ALU.add).then_inc(s_aff, 1)

            stages = {
                4: {3: [centre(0), normalise(0)]},
                5: {3: [centre(0), normalise(0)]},
                6: {6: [centre(0)], 7: [normalise(0), affine], 12: [centre(1)], 13: [normalise(1)]},
                8: {5: [centre(0), normalise(0), store]},
            }
            at = 0

            pool.wait_ge(s_alo, RING)
            for dst, src in small:
                pool.dma_start(dst, src).then_inc(s_small, 16)
            pool.wait_ge(s_alo, STEPS * NC)
            pool.dma_start(x_rows[:, :, :], x).then_inc(s_x, 16)
            for st in STREAM[GATED_FROM:GATED_FROM + STEPS * NC]:
                for s in range(SJ):
                    u = gated_index(st, s)
                    at = epilogue(stages, at, freed(st) + s)
                    if u % ACT_SQUARES == ACT_SQUARES - 1:
                        continue
                    pool.wait_ge(s_a[st.n % RING], 16 * (st.n // RING + 1))
                    adj_block = slot(a_ring, st)[:, s, :]
                    pool.tensor_tensor(adj_block, adj_block, adj_block, ALU.mult).then_inc(s_sq, 1)
            epilogue(stages, at, THE_END)


def kernel(**inputs):
    import numpy as np
    import concourse.bacc as bacc
    from concourse.bass_utils import run_bass_kernel_spmd

    def columns(v):
        return np.ascontiguousarray(v.reshape(NB, P).T)

    adj = np.asarray(inputs["adj"])
    x = np.asarray(inputs["x"])
    laid_out = {
        "adj": np.ascontiguousarray(adj.reshape(NC, CH, STEPS, SJ, P).transpose(0, 2, 4, 3, 1)),
        "x": np.ascontiguousarray(x.reshape(NB, P, F).transpose(1, 0, 2)),
        "xt": np.ascontiguousarray(x.T),
        "W1": np.asarray(inputs["L0_gnn_W1"]), "f1": columns(np.asarray(inputs["L0_gnn_f1"])),
        "W2": np.asarray(inputs["L0_gnn_W2"]), "f2": columns(np.asarray(inputs["L0_gnn_f2"])),
        "Wcat": np.asarray(inputs["L1_gnn_weight"]),
        "W_msg": np.asarray(inputs["L2_gnn_W_msg"]), "b_msg": np.asarray(inputs["L2_gnn_b_msg"]),
        "W_qT": np.ascontiguousarray(np.asarray(inputs["L2_gnn_W_q"]).T),
        "W_kT": np.ascontiguousarray(np.asarray(inputs["L2_gnn_W_k"]).T),
        "gate_bias": np.asarray(inputs["L2_gnn_gate_bias"]).reshape(1),
        "W_upd": np.asarray(inputs["L2_gnn_W_upd"]), "b_upd": np.asarray(inputs["L2_gnn_b_upd"]),
        "ln_g": np.asarray(inputs["L2_gnn_ln_gamma"]), "ln_b": np.asarray(inputs["L2_gnn_ln_beta"]),
        "W3": np.asarray(inputs["L3_gnn_W"]), "b3": np.asarray(inputs["L3_gnn_b"]),
    }
    nc = bacc.Bacc("TRN2", target_bir_lowering=False, num_devices=1)
    arrays, args = {}, {}
    for name, a in laid_out.items():
        arrays[f"{name}_dram"] = a
        args[name] = nc.dram_tensor(f"{name}_dram", a.shape, mybir.dt.from_np(a.dtype), kind="ExternalInput").ap()
    args["out"] = nc.dram_tensor("out_dram", (P, NB, F), F32, kind="ExternalOutput").ap()
    build(nc, **args)
    r = run_bass_kernel_spmd(nc, [arrays], core_ids=[0])
    return np.ascontiguousarray(r.results[0]["out_dram"].transpose(1, 0, 2)).reshape(N, F)
```

```python
from collections import namedtuple
from contextlib import ExitStack

import concourse.bass as bass
from concourse import mybir

P = 128
N = 4096
F = 128
NB = N // P
CH = 1024
NC = N // CH
CB = CH // P
SJ = 2
STEPS = NB // SJ
LOADS = 5
RING = 4
BANK = 512
HALVES = CH // BANK
HB = CB // HALVES
PASSES = 8
GATED = 6
AHEAD = 4
LONE_LOGITS = 5
ACT_SQUARES = 8

A_EXP = 10
G_EXP = 12
Y_EXP = [3, -2, 0, -5, 5, 2, 5, 5]
Q_EXP, K_EXP = -3, 4
LN_EPS = 1e-5
RSQRT_GUESS = 0x5F3759DF
G_RING = 4
NEWTON = 3

ALU = mybir.AluOpType
ACT = mybir.ActivationFunctionType
AX = mybir.AxisListType.X
F32 = mybir.dt.float32
F16 = mybir.dt.float16

UP, DOWN = [0, 1, 2, 3], [3, 2, 1, 0]
ORDER = {0: UP, 1: UP, 2: DOWN, 3: UP, 4: DOWN, 5: UP, 6: UP, 7: UP, 8: DOWN}
WHOLE = (1, 7)
HALF = (2, 3, 4, 5, 8)
AHEAD_OF = (1, 2, 3, 4, 7)
LATE = (4,)

PER_CHUNK = {
    "rows": {0: 1, 1: 1, 2: 1, 3: 1, 4: 2, 5: 5, 6: 1, 7: 2, 8: 2},
    "x_T": {4: 1, 5: 1},
    "relu_z": {2: 1},
    "val": {1: 1, 3: 1, 4: 1, 5: 1, 6: 1},
    "nonlin": {6: 1, 7: 1, 8: 1},
    "swished": {7: 1, 8: 1},
    "resid": {6: 1, 8: 1},
    "affine": {6: 2},
    "ln": {4: 1, 5: 1, 6: 2, 8: 1},
    "msg": {5: 1},
    "qk": {5: 2},
}


def nth(stage, p, k, run=0):
    per = PER_CHUNK[stage]
    return NC * sum(n for q, n in per.items() if q < p) + per[p] * k + run + 1


OWN, BOTH, TAIL = "own", "own and next, step by step", "own, then next"
GROUP = STEPS // NC
Block = namedtuple("Block", "p k i j mode")


def blocks_of(p):
    o = ORDER[p]
    both, last = (BOTH, TAIL) if p in AHEAD_OF else (OWN, OWN)
    if p == GATED:
        at = [(k, j, OWN) for k in range(NC) for j in range(NC)]
    elif p in WHOLE:
        at = [(0, 0, OWN), (0, 1, OWN), (0, 2, OWN), (1, 1, OWN), (0, 3, OWN), (1, 2, OWN), (1, 3, OWN), (1, 0, both),
              (2, 2, OWN), (2, 3, OWN), (2, 0, both), (2, 1, both), (3, 3, OWN), (3, 0, both), (3, 1, both),
              (3, 2, last)]
    else:
        at = [(1, 1, OWN), (0, 0, OWN), (1, 0, OWN if p in LATE else last), (2, 2, OWN), (2, 0, both), (2, 1, both),
              (3, 3, OWN), (3, 0, both), (3, 1, both), (3, 2, last)]
        if p - 1 in LATE:
            at.insert(3, (2, 3, OWN))
    return [Block(p, k, o[k], o[j], mode) for k, j, mode in at]


Step = namedtuple("Step", "n p k i j0")
Unit = namedtuple("Unit", "step use s first last")


def plan():
    steps, units = [], []
    for p in range(1, PASSES + 1):
        for b in blocks_of(p):
            group = [Step(len(steps) + t, p, b.k, b.i, (b.j * GROUP + t) * SJ) for t in range(GROUP)]
            steps += group
            if p == GATED:
                units += [(st, "own", s) for st in group for s in range(SJ)]
            elif b.mode == BOTH:
                units += [(st, use, None) for st in group for use in ("own", "next")]
            else:
                units += [(st, "own", None) for st in group]
                if b.mode == TAIL:
                    units += [(st, "next", None) for st in group]
    key = [(st.p, st.k, use) for st, use, _ in units]
    first, last = {}, {}
    for n, x in enumerate(key):
        first.setdefault(x, n)
        last[x] = n
    return steps, [Unit(st, use, s, first[x] == n, last[x] == n) for n, ((st, use, s), x) in enumerate(zip(units, key))]


STREAM, UNITS = plan()
FIRST_USE, LAST_USE, SUM_DONE = {}, {}, {}
for _n, _u in enumerate(UNITS):
    FIRST_USE.setdefault(_u.step.n, _n)
    LAST_USE[_u.step.n] = _n
    SUM_DONE[_u.step.p, _u.step.k, _u.use] = _n
PLAIN_BEFORE = [sum(st.p != GATED for st in STREAM[:n]) for n in range(len(STREAM) + 1)]
GATED_FROM = PLAIN_BEFORE.index(PLAIN_BEFORE[-1] - sum(st.p > GATED for st in STREAM))
SAVED = sorted((p, k) for p, k, use in SUM_DONE if use == "next")

LAST_GATED = 10 + GATED
LENGTH = {0: 1, 1: 4, 2: 3, 3: 3, 4: 7, 5: 10, 6: 23, 7: 4, 8: 9, LAST_GATED: 14}


def timing(p, k):
    return LAST_GATED if (p, k) == (GATED, NC - 1) else p


def epilogues():
    out = [(0, k, k) for k in range(NC)]
    for p in range(1, PASSES + 1):
        for k in range(NC):
            q, kk, before = out[-1]
            out.append((p, k, max(SUM_DONE[p, k, "own"] + 1, before + LENGTH[timing(q, kk)])))
    return out[:-1]


EPILOGUES = epilogues()


def epilogue_by_unit():
    at = {}
    for p, k in SAVED:
        at.setdefault(SUM_DONE[p, k, "next"] + 1, []).append((p, k, "save"))
    for p, k, start in EPILOGUES:
        for t in range(LENGTH[timing(p, k)] + 1):
            at.setdefault(start + t, []).append((p, k, t))
    return at


DUE_AT = epilogue_by_unit()
THE_END = max(DUE_AT)


def build(nc, adj, x, xt, W1, f1, W2, f2, Wcat, W_msg, b_msg, W_qT, W_kT, gate_bias, W_upd, b_upd, ln_g,
          ln_b, W3, b3, out):
    with ExitStack() as ctx:
        def sb(name, shape, dt=F32):
            return ctx.enter_context(nc.sbuf_tensor(name, shape, dt))

        def sem(name):
            return ctx.enter_context(nc.semaphore(name))

        a_ring = sb("a_ring", [P, LOADS, SJ, CH])
        a_hi = sb("a_hi", [P, RING, SJ, CH], F16)
        a_lo = sb("a_lo", [P, RING, SJ, CH], F16)
        y_hi = sb("y_hi", [P, 2, N], F16)
        y_lo = sb("y_lo", [P, 2, N], F16)
        x_rows = sb("x_rows", [P, NB, F])
        x_T = sb("x_T", [P, N])
        qT_hi, qT_lo = sb("qT_hi", [P, N], F16), sb("qT_lo", [P, N], F16)
        kT_hi, kT_lo = sb("kT_hi", [P, N], F16), sb("kT_lo", [P, N], F16)
        gates = sb("gates", [P, G_RING, CH])
        z_T = sb("z_T", [P, CH])
        val = sb("val", [P, CB, F])
        tmp = sb("tmp", [P, CB, F])
        tmp_T = tmp[:, :, :].rearrange("p b f -> p (b f)")
        xn = sb("xn", [P, CB, F])
        xn_T = xn[:, :, :].rearrange("p b f -> p (b f)")
        bn = sb("bn", [P, CB, 6])
        moments = sb("moments", [P, CB, 2])
        stats = sb("stats", [P, 3, CB])
        ident = sb("ident", [P, P])
        w1, w2, w3 = sb("w1", [P, F]), sb("w2", [P, F]), sb("w3", [P, F])
        wcat, wupd = sb("wcat", [P, 2, F]), sb("wupd", [P, 2, F])
        wmsg, w_qk = sb("wmsg", [P, F]), sb("w_qk", [P, F])
        wqT, wkT = tmp[:, 0, :], tmp[:, 1, :]
        f1c, f2c = sb("f1c", [P, NB]), sb("f2c", [P, NB])
        bmsg, gbias, b3c = sb("bmsg", [P, 1]), sb("gbias", [P, 1]), sb("b3c", [P, 1])
        bupd, gam, bet = sb("bupd", [P, F]), sb("gam", [P, F]), sb("bet", [P, F])

        acc = ctx.enter_context(nc.psum_tensor("acc", [P, 2, CH], F32))
        spare = ctx.enter_context(nc.psum_tensor("spare", [P, CH], F32))
        rows = ctx.enter_context(nc.psum_tensor("rows", [P, CB, F], F32))

        s_small = sem("small_loaded")
        s_w1, s_x = sem("w1_loaded"), sem("x_loaded")
        s_xt = [sem(f"xt_loaded{i}") for i in range(NC)]
        s_a = [sem(f"a_loaded{i}") for i in range(LOADS)]
        s_id0, s_id = sem("ident_zero"), sem("ident_ready")
        s_ahi, s_alo, s_unit = sem("a_hi_ready"), sem("a_lo_ready"), sem("unit_multiplied")
        s_lg, s_pr = sem("logits_ready"), sem("probs_ready")
        s_sq, s_sqa = sem("squares_by_gpsimd"), sem("squares_by_scalar")
        s_g, s_ghi, s_glo = sem("gates_ready"), sem("g_hi_ready"), sem("g_lo_ready")
        s_rows, s_xT = sem("rows_written"), sem("x_T_saved")
        s_zt, s_val, s_nl, s_sw = sem("z_T_ready"), sem("val_ready"), sem("nonlinearity_done"), sem("swish_done")
        s_res, s_aff = sem("residual_added"), sem("affine_done")
        s_bn, s_moments, s_var = sem("ln_bn"), sem("ln_moments"), sem("ln_var")
        s_cen, s_ln = sem("ln_centred"), sem("ln_done")
        s_guess, s_newton = sem("ln_guess"), sem("ln_newton")
        s_yhi, s_y = sem("y_hi_ready"), sem("y_ready")
        s_saved, s_zrelu = sem("next_sums_saved"), sem("z_T_relu_done")
        s_wqk_product, s_wqk = sem("w_qk_product"), sem("w_qk_ready")
        s_msg, s_qkhi, s_qk = sem("m_T_ready"), sem("qk_hi_ready"), sem("qk_ready")
        s_half, s_out, s_last_out = sem("half_of_last_multiplied"), sem("out_stored"), sem("last_halves_stored")

        small = [(w2[:], W2), (w3[:], W3), (wmsg[:], W_msg), (wqT, W_qT),
                 (wkT, W_kT), (wcat[:, :, :], Wcat.rearrange("(t k) n -> k t n", t=2)),
                 (wupd[:, :, :], W_upd.rearrange("(t k) n -> k t n", t=2)), (f1c[:], f1), (f2c[:], f2),
                 (bmsg[:], b_msg.rearrange("(k a) -> k a", a=1)), (gbias[:], gate_bias.partition_broadcast(P)),
                 (bupd[:], b_upd.partition_broadcast(P)), (gam[:], ln_g.partition_broadcast(P)),
                 (bet[:], ln_b.partition_broadcast(P)), (b3c[:], b3.rearrange("(k a) -> k a", a=1))]
        SMALL = 16 * len(small)

        def blk(t, b):
            return t[:, b * P:(b + 1) * P]

        def over_blocks(v):
            return v[:, :].unsqueeze(1).to_broadcast([P, CB, F])

        def over_features(v):
            return v.unsqueeze(2).to_broadcast([P, CB, F])

        def normalised(p, k, run=0):
            return xn[:, :, :] if p == GATED and run == 0 else x_chunk(p, k)

        def x_chunk(p, k):
            i = ORDER[p][k]
            return x_rows[:, i * CB:(i + 1) * CB, :]

        def x_T_chunk(p, k):
            i = ORDER[p][k]
            return x_T[:, i * CH:(i + 1) * CH]

        def y_chunk(y, p, k):
            i = ORDER[p][k]
            return y[:, p % 2, i * CH:(i + 1) * CH]

        def flat(v):
            return v.rearrange("p b f -> p (b f)")

        def y_ready(p, j):
            return NC * p + ORDER[p].index(j) + 1

        def epilogue(stages, since, until):
            for n in range(since, until + 1):
                for p, k, t in DUE_AT.get(n, []):
                    for stage in stages.get(timing(p, k), {}).get(t, []):
                        stage(p, k)
            return max(since, until + 1)

        def freed(st):
            return LAST_USE[st.n - RING] + 1 if st.n >= RING else 0

        def loaded(st):
            return a_ring[:, st.n % LOADS, :, :]

        def slot(t, st):
            return t[:, st.n % RING, :, :]

        def half(v, h):
            return v[:, h * HB:(h + 1) * HB, :]

        def half_T(v, h):
            return v[:, h * BANK:(h + 1) * BANK]

        def last(stage, n):
            return nth(stage, PASSES, NC - 1) - 1 + n

        def part(i):
            return gates[:, i, :]

        def gated_index(st, s):
            return (st.n - GATED_FROM) * SJ + s

        def in_idle_sums(u):
            return u % NB >= LONE_LOGITS and (u - LONE_LOGITS) % 2 == 0

        def logits_of(u):
            return acc[:, (u // NB + 1) % 2, :] if in_idle_sums(u) else spare[:, :]

        def logits_before(u):
            v = u - 1
            while v >= 0 and in_idle_sums(v) != in_idle_sums(u):
                v -= 1
            return v if in_idle_sums(u) is False or v // NB == u // NB else -1

        def takes_over(p, k):
            return (p - 1, NC - 1 - k) in SAVED

        def back(p):
            return 2.0 ** -((G_EXP if p == GATED else A_EXP) + Y_EXP[p - 1])

        def buffers_free(eng, p, k):
            if p == PASSES and k:
                eng.wait_ge(s_ln, nth("ln", p, k - 1))
            else:
                eng.wait_ge(s_y, NC * p + k)
            if p in (4, 5) and (p, k) != (4, 0):
                q, kk = (p, k - 1) if k else (p - 1, NC - 1)
                eng.wait_ge(s_xT, nth("x_T", q, kk))

        def y_source(p, k):
            if p in (0, 2, 5, 7):
                return flat(rows[:, :, :])
            return flat(val[:, :, :]) if p in (1, 3) else flat(normalised(p, k, 1))

        block = ctx.enter_context(nc.Block())

        @block.sync
        def _(sp):
            def load(st):
                if st.n >= LOADS:
                    before = STREAM[st.n - LOADS]
                    if before.p == GATED:
                        sp.wait_ge(s_g, gated_index(before, SJ - 1) + 1)
                    else:
                        sp.wait_ge(s_alo, PLAIN_BEFORE[before.n] + 1)
                sp.dma_start(loaded(st), adj[st.i, st.j0 // SJ]).then_inc(s_a[st.n % LOADS], 16)

            for ic in range(NC):
                sp.dma_start(x_T[:, ic * CH:(ic + 1) * CH], xt[:, ic * CH:(ic + 1) * CH]).then_inc(s_xt[ic], 16)
                load(STREAM[ic])
            for st in STREAM[NC:]:
                load(st)
            for h in range(HALVES):
                sp.wait_ge(s_ln, last("ln", h + 1))
                first = ORDER[PASSES][NC - 1] * CB + h * HB
                sp.dma_start(out[:, first:first + HB, :], x_rows[:, first:first + HB, :]).then_inc(s_last_out, 16)
            sp.wait_ge(s_out, 16 * (NC - 1))
            sp.wait_ge(s_last_out, 16 * HALVES)

        @block.tensor
        def _(pe):
            def transposes(source):
                for b in range(CB):
                    last = pe.transpose(rows[:, b, :], source(b), ident[:, :])
                last.then_inc(s_rows, 1)

            def by_node(*terms):
                for b in range(CB):
                    for t, (left, right) in enumerate(terms):
                        last = pe.matmul(rows[:, b, :], blk(left, b), right, start=(t == 0), stop=(t == len(terms) - 1))
                last.then_inc(s_rows, 1)

            def by_feature(weight, right):
                for h in range(HALVES):
                    last = pe.matmul(flat(rows[:, :, :])[:, h * BANK:(h + 1) * BANK], weight,
                                     right[:, h * BANK:(h + 1) * BANK], start=True, stop=True)
                last.then_inc(s_rows, 1)

            def project(p, k):
                if p == 0:
                    pe.wait_ge(s_xt[k], 16)
                    if k:
                        pe.wait_ge(s_y, k)
                elif p == 2:
                    pe.wait_ge(s_zrelu, nth("relu_z", p, k))
                else:
                    pe.wait_ge(s_zt, NC * (p - 1) + k + 1)
                if p == 1 and k == 0:
                    pe.wait_ge(s_id, 1)
                    pe.wait_ge(s_small, SMALL)
                if p in (1, 3, 4):
                    transposes(lambda b: blk(z_T, b))
                elif p == 5:
                    by_node((x_T_chunk(p, k), wcat[:, 0, :]), (z_T, wcat[:, 1, :]))
                elif p == 6:
                    by_node((x_T_chunk(p, k), wupd[:, 0, :]), (z_T, wupd[:, 1, :]))
                elif p == 0:
                    by_node((x_T_chunk(p, k), w1[:, :]))
                elif p == 2:
                    by_node((z_T, w2[:, :]))
                else:
                    by_feature(w3[:], z_T)

            def swished_rows(p, k):
                pe.wait_ge(s_sw, nth("swished", p, k))
                transposes(lambda b: blk(xn_T, b))

            def x_transposes(p, k):
                pe.wait_ge(s_ln, nth("ln", p, k))
                transposes(lambda b: normalised(p, k)[:, b, :])

            def messages(p, k):
                pe.wait_ge(s_xT, nth("x_T", p, k))
                by_feature(wmsg[:], x_T_chunk(p, k))

            def query_key_weights(p, k):
                if k == 0:
                    pe.wait_ge(s_small, SMALL)
                    pe.matmul(spare[:, :F], wqT, wkT, start=True, stop=True).then_inc(s_wqk_product, 1)

            def queries(p, k):
                pe.wait_ge(s_msg, nth("msg", p, k))
                by_feature(w_qk[:], tmp_T)

            def message_rows(p, k):
                pe.wait_ge(s_qk, nth("qk", p, k, 1))
                transposes(lambda b: blk(tmp_T, b))

            stages = {
                0: {0: [project]},
                1: {2: [project, query_key_weights]},
                2: {2: [project]},
                3: {1: [project]},
                4: {1: [project], 7: [x_transposes]},
                5: {1: [project], 5: [x_transposes], 6: [messages], 7: [queries], 9: [message_rows]},
                6: {3: [project]},
                7: {1: [project], 3: [swished_rows]},
                8: {2: [project], 3: [swished_rows]},
                LAST_GATED: {1: [project]},
            }
            at = 0

            def product(unit, s, halves=range(HALVES)):
                st = unit.step
                y_pass = st.p - 1 if unit.use == "own" else st.p
                sums = acc[:, st.k % 2, :] if unit.use == "own" else spare[:, :]
                j = st.j0 + s
                begins = unit.first and s == (unit.s or 0)
                ends = unit.last and s == SJ - 1
                for t, (y, a) in enumerate([(y_hi, a_hi), (y_hi, a_lo), (y_lo, a_hi)]):
                    for h in halves:
                        mm = pe.matmul(sums[:, h * BANK:(h + 1) * BANK], blk(y[:, y_pass % 2, :], j),
                                       slot(a, st)[:, s, h * BANK:(h + 1) * BANK],
                                       start=(begins and t == 0), stop=(ends and t == 2))
                return mm

            def logit(u):
                st = STREAM[GATED_FROM + u // SJ]
                j = st.j0 + u % SJ
                before = logits_before(u)
                if before >= 0:
                    pe.wait_ge(s_pr, before + 1)
                if u % NB == LONE_LOGITS:
                    pe.wait_ge(s_zt, NC * (GATED - 1) + st.k)
                if j % CB == 0 and st.k == 0:
                    pe.wait_ge(s_qk, nth("qk", 5, ORDER[5].index(j // CB), 1 if u == 0 else 0))
                if j % CB == 0 and st.j0 // CB == ORDER[GATED][0] and st.k:
                    pe.wait_ge(s_qk, nth("qk", 5, ORDER[5].index(st.i), 1))
                for t, (k, q) in enumerate([(kT_hi, qT_hi), (kT_hi, qT_lo), (kT_lo, qT_hi)]):
                    for h in range(HALVES):
                        mm = pe.matmul(logits_of(u)[:, h * BANK:(h + 1) * BANK], blk(k, j),
                                       q[:, st.i * CH + h * BANK:st.i * CH + (h + 1) * BANK],
                                       start=(t == 0), stop=(t == 2))
                mm.then_inc(s_lg, 1)

            pe.wait_ge(s_w1, 16)
            for n, unit in enumerate(UNITS[:-GROUP]):
                at = epilogue(stages, at, n)
                if 0 <= n - FIRST_USE[GATED_FROM] + AHEAD < NB * NC:
                    logit(n - FIRST_USE[GATED_FROM] + AHEAD)
                st = unit.step
                if st.p == GATED:
                    u = gated_index(st, unit.s)
                    pe.wait_ge(s_glo, u + 1)
                elif FIRST_USE[st.n] == n:
                    pe.wait_ge(s_alo, PLAIN_BEFORE[st.n] + 1)
                if unit.first and unit.use == "own" and (st.p, st.k) not in ((1, 0), (1, 1)):
                    pe.wait_ge(s_zt, NC * (st.p - 1) + st.k - 1)
                if unit.first and unit.use == "next" and not SAVED.index((st.p, st.k)):
                    pe.wait_ge(s_wqk, 1)
                if unit.first and unit.use == "next" and SAVED.index((st.p, st.k)):
                    pe.wait_ge(s_saved, SAVED.index((st.p, st.k)))
                if st.j0 % CB == 0 and not unit.s:
                    pe.wait_ge(s_y, y_ready(st.p - 1 if unit.use == "own" else st.p, st.j0 // CB))
                for s in range(SJ) if unit.s is None else [unit.s]:
                    mm = product(unit, s)
                mm.then_inc(s_unit, 1)
            epilogue(stages, at, THE_END)

            def half_step(t, h):
                unit = UNITS[t - GROUP]
                if h == 0:
                    pe.wait_ge(s_alo, PLAIN_BEFORE[unit.step.n] + 1)
                for s in range(SJ):
                    mm = product(unit, s, [h])
                return mm

            def project_half(h):
                pe.wait_ge(s_zt, NC * PASSES - 1 + h + 1)
                pe.matmul(half_T(flat(rows[:, :, :]), h), w3[:], half_T(z_T, h), start=True,
                          stop=True).then_inc(s_rows, 1)

            def swished_half(h):
                pe.wait_ge(s_sw, last("swished", h + 1))
                for b in range(h * HB, (h + 1) * HB):
                    mm = pe.transpose(rows[:, b, :], blk(xn_T, b), ident[:, :])
                mm.then_inc(s_rows, 1)

            for t, h in [(0, 0), (1, 0), (0, 1), (2, 0), (1, 1)]:
                half_step(t, h)
            half_step(3, 0).then_inc(s_half, 1)
            half_step(2, 1)
            project_half(0)
            half_step(3, 1).then_inc(s_half, 1)
            swished_half(0)
            project_half(1)
            swished_half(1)

        @block.scalar
        def _(act):
            act.dma_start(w1[:], W1).then_inc(s_w1, 16)

            def evacuate(p, k):
                if not takes_over(p, k):
                    act.wait_ge(s_unit, SUM_DONE[p, k, "own"] + 1)
                    buffers_free(act, p, k)
                    act.activation(z_T[:, :], acc[:, k % 2, :], ACT.Copy, scale=back(p)).then_inc(s_zt, 1)

            def save_sums(p, k):
                i = ORDER[p][k]
                act.wait_ge(s_unit, SUM_DONE[p, k, "next"] + 1)
                act.wait_ge(s_zt, NC * (p - 1) + k + 1)
                act.activation(part(i), spare[:, :], ACT.Copy, scale=back(p + 1)).then_inc(s_saved, 1)

            def relu_z(p, k):
                act.wait_ge(s_zt, NC * (p - 1) + k + 1)
                act.activation(z_T[:, :], z_T[:, :], ACT.Relu).then_inc(s_zrelu, 1)

            def y_high(p, k):
                if p in (0, 2, 5, 7):
                    act.wait_ge(s_rows, nth("rows", p, k, PER_CHUNK["rows"][p] - 1))
                elif p in (1, 3):
                    act.wait_ge(s_val, nth("val", p, k))
                else:
                    act.wait_ge(s_ln, nth("ln", p, k, PER_CHUNK["ln"][p] - 1))
                act.activation(y_chunk(y_hi, p, k), y_source(p, k), ACT.Copy, scale=2.0 ** Y_EXP[p]).then_inc(s_yhi, 1)

            def save_x_T(p, k):
                act.wait_ge(s_rows, nth("rows", p, k, 1))
                act.activation(x_T_chunk(p, k), flat(rows[:, :, :]), ACT.Copy).then_inc(s_xT, 1)

            def save_m_T(p, k):
                act.wait_ge(s_rows, nth("rows", p, k, 2))
                act.activation(tmp_T, flat(rows[:, :, :]), ACT.Identity, bias=bmsg[:, 0:1]).then_inc(s_msg, 1)

            def save_w_qk(p, k):
                if k == 0:
                    act.wait_ge(s_wqk_product, 1)
                    act.activation(w_qk[:], spare[:, :F], ACT.Copy).then_inc(s_wqk, 1)

            def qk_high(run, dst, exp):
                def go(p, k):
                    i = ORDER[p][k]
                    if run:
                        act.wait_ge(s_rows, nth("rows", p, k, 3))
                    else:
                        act.wait_ge(s_msg, nth("msg", p, k))
                    act.activation(dst[:, i * CH:(i + 1) * CH], flat(rows[:, :, :]) if run else tmp_T, ACT.Copy,
                                   scale=2.0 ** exp).then_inc(s_qkhi, 1)
                return go

            def relu(p, k):
                act.wait_ge(s_val, nth("val", p, k))
                act.activation(val[:, :, :], val[:, :, :], ACT.Relu).then_inc(s_nl, 1)

            def sigmoid(p, k):
                act.wait_ge(s_rows, nth("rows", p, k))
                act.activation(tmp_T, flat(rows[:, :, :]), ACT.Sigmoid, bias=b3c[:, 0:1]).then_inc(s_nl, 1)

            stages = {
                0: {0: [y_high]},
                1: {0: [evacuate], 1: [save_w_qk], 2: [y_high]},
                2: {0: [evacuate, relu_z], 2: [y_high]},
                3: {0: [evacuate], 2: [y_high]},
                4: {0: [evacuate], 5: [y_high], 7: [save_x_T]},
                5: {0: [evacuate], 5: [save_x_T], 6: [save_m_T], 7: [qk_high(0, kT_hi, K_EXP)],
                    8: [qk_high(1, qT_hi, Q_EXP)], 9: [y_high]},
                6: {1: [evacuate], 6: [relu], 23: [y_high]},
                7: {0: [evacuate], 2: [sigmoid], 3: [y_high]},
                8: {0: [evacuate], 2: [sigmoid]},
                LAST_GATED: {0: [evacuate], 3: [relu], 14: [y_high]},
            }
            for p in AHEAD_OF:
                stages[p]["save"] = [save_sums]
            at = 0

            def split_high(st):
                act.wait_ge(s_a[st.n % LOADS], 16 * (st.n // LOADS + 1))
                if st.n >= RING:
                    act.wait_ge(s_unit, freed(st))
                act.activation(slot(a_hi, st), loaded(st), ACT.Copy, scale=2.0 ** A_EXP).then_inc(s_ahi, 1)

            def gate_high(u):
                st = STREAM[GATED_FROM + u // SJ]
                act.wait_ge(s_g, u + 1)
                before = STREAM[st.n - RING]
                act.wait_ge(s_unit, LAST_USE[before.n] + 1 - (SJ - 1 - u % SJ if before.p == GATED else 0))
                act.activation(slot(a_hi, st)[:, u % SJ, :], gates[:, u % G_RING, :], ACT.Copy).then_inc(s_ghi, 1)

            for st in STREAM:
                if st.p != GATED:
                    at = epilogue(stages, at, freed(st))
                    split_high(st)
                    continue
                for s in range(SJ):
                    u = gated_index(st, s)
                    at = epilogue(stages, at, FIRST_USE[st.n] + s - AHEAD + 1)
                    if u % ACT_SQUARES == ACT_SQUARES - 1:
                        act.wait_ge(s_a[st.n % LOADS], 16 * (st.n // LOADS + 1))
                        act.activation(loaded(st)[:, s, :], loaded(st)[:, s, :], ACT.Square).then_inc(s_sqa, 1)
                    act.wait_ge(s_lg, u + 1)
                    if u >= G_RING:
                        act.wait_ge(s_glo, u - G_RING + 1)
                    elif u == 0:
                        act.wait_ge(s_zt, NC * (GATED - 1) - 1)
                    act.activation(gates[:, u % G_RING, :], logits_of(u), ACT.Sigmoid, bias=gbias[:, 0:1],
                                   scale=2.0 ** -(Q_EXP + K_EXP) * F ** -0.5).then_inc(s_pr, 1)
                    if u >= 1:
                        gate_high(u - 1)
                    if u == NB * NC - 1:
                        gate_high(u)
            epilogue(stages, at, THE_END)
            for h in range(HALVES):
                act.wait_ge(s_half, h + 1)
                if h == 0:
                    buffers_free(act, PASSES, NC - 1)
                act.activation(half_T(z_T, h), half_T(acc[:, (NC - 1) % 2, :], h), ACT.Copy,
                               scale=back(PASSES)).then_inc(s_zt, 1)
                act.wait_ge(s_rows, last("rows", 1 if h == 0 else 3))
                act.activation(half_T(tmp_T, h), half_T(flat(rows[:, :, :]), h), ACT.Sigmoid,
                               bias=b3c[:, 0:1]).then_inc(s_nl, 1)

        @block.vector
        def _(dve):
            def take_over(p, k):
                if takes_over(p, k):
                    i = ORDER[p][k]
                    dve.wait_ge(s_unit, SUM_DONE[p, k, "own"] + 1)
                    buffers_free(dve, p, k)
                    dve.wait_ge(s_saved, SAVED.index((p - 1, ORDER[p - 1].index(i))) + 1)
                    dve.scalar_tensor_tensor(out=z_T[:, :], in0=acc[:, k % 2, :], scalar=back(p), in1=part(i),
                                             op0=ALU.mult, op1=ALU.add).then_inc(s_zt, 1)

            def y_low(p, k):
                dve.wait_ge(s_yhi, NC * p + k + 1)
                dve.scalar_tensor_tensor(out=y_chunk(y_lo, p, k), in0=y_source(p, k), scalar=2.0 ** Y_EXP[p],
                                         in1=y_chunk(y_hi, p, k), op0=ALU.mult, op1=ALU.subtract).then_inc(s_y, 1)

            def values(p, k):
                i = ORDER[p][k]
                dve.wait_ge(s_rows, nth("rows", p, k))
                if p == 1 and k == 0:
                    dve.wait_ge(s_small, SMALL)
                if p == 4 and k == 0:
                    dve.wait_ge(s_x, 16)
                if p in (1, 3):
                    right, op = over_features((f1c if p == 1 else f2c)[:, i * CB:(i + 1) * CB]), ALU.mult
                elif p in (4, 5):
                    right, op = x_chunk(p, k), ALU.add
                else:
                    right, op = over_blocks(bupd), ALU.add
                dve.tensor_tensor(val[:, :, :], rows[:, :, :], right, op).then_inc(s_val, 1)

            def swish(p, k):
                dve.wait_ge(s_nl, nth("nonlin", p, k))
                dve.scalar_tensor_tensor(out=xn_T, in0=flat(rows[:, :, :]), scalar=b3c[:, 0:1], in1=tmp_T, op0=ALU.add,
                                         op1=ALU.mult).then_inc(s_sw, 1)

            def residual(p, k):
                if p == GATED:
                    dve.wait_ge(s_aff, nth("affine", p, k, 1))
                else:
                    dve.wait_ge(s_rows, nth("rows", p, k, 1))
                update = xn if p == GATED else rows
                dve.tensor_tensor(val[:, :, :], update[:, :, :], x_chunk(p, k), ALU.add).then_inc(s_res, 1)

            def moments_of(blocks, before):
                for b in blocks:
                    dve.bn_stats(bn[:, b, :], val[:, b, :]).then_inc(s_bn, 1)
                dve.wait_ge(s_bn, before + len(blocks))
                for b in blocks:
                    dve.bn_aggr(moments[:, b, :], bn[:, b, :]).then_inc(s_moments, 1)

            def rstd_of(blocks, moments_done, n):
                var, r, t = [stats[:, v, blocks[0]:blocks[-1] + 1] for v in range(3)]
                as_int = lambda v: v.bitcast(mybir.dt.int32)
                dve.wait_ge(s_moments, moments_done)
                dve.tensor_scalar(var, moments[:, blocks[0]:blocks[-1] + 1, 1], LN_EPS, None,
                                  ALU.add).then_inc(s_var, 1)
                dve.wait_ge(s_var, n)
                dve.tensor_scalar(as_int(r), as_int(var), -0.5, float(RSQRT_GUESS), ALU.mult,
                                  ALU.add).then_inc(s_guess, 1)
                dve.wait_ge(s_guess, n)
                for step in range(NEWTON):
                    done = 3 * (NEWTON * (n - 1) + step)
                    if step:
                        dve.wait_ge(s_newton, done)
                    dve.tensor_tensor(t, r, r, ALU.mult).then_inc(s_newton, 1)
                    dve.wait_ge(s_newton, done + 1)
                    dve.scalar_tensor_tensor(out=t, in0=t, scalar=-0.5, in1=var, op0=ALU.mult,
                                             op1=ALU.mult).then_inc(s_newton, 1)
                    dve.wait_ge(s_newton, done + 2)
                    dve.scalar_tensor_tensor(out=r, in0=t, scalar=1.5, in1=r, op0=ALU.add,
                                             op1=ALU.mult).then_inc(s_newton, 1)

            def ln_moments(run, ready, stage):
                def go(p, k):
                    dve.wait_ge(ready, nth(stage, p, k))
                    moments_of(range(CB), CB * (nth("ln", p, k, run) - 1))
                return go

            def ln_rstd(run):
                def go(p, k):
                    n = nth("ln", p, k, run)
                    rstd_of(range(CB), CB * n, n)
                return go

            def qk_low(run, hi, lo, exp):
                def go(p, k):
                    i = ORDER[p][k]
                    dve.wait_ge(s_qkhi, nth("qk", p, k, run))
                    dve.scalar_tensor_tensor(out=lo[:, i * CH:(i + 1) * CH],
                                             in0=flat(rows[:, :, :]) if run else tmp_T, scalar=2.0 ** exp,
                                             in1=hi[:, i * CH:(i + 1) * CH], op0=ALU.mult,
                                             op1=ALU.subtract).then_inc(s_qk, 1)
                return go

            stages = {
                0: {0: [y_low]},
                1: {0: [take_over], 1: [values], 2: [y_low]},
                2: {0: [take_over], 2: [y_low]},
                3: {0: [take_over], 1: [values], 2: [y_low]},
                4: {0: [take_over], 1: [values, ln_moments(0, s_val, "val"), ln_rstd(0)], 5: [y_low]},
                5: {0: [take_over], 1: [values], 2: [ln_moments(0, s_val, "val"), ln_rstd(0)],
                    7: [qk_low(0, kT_hi, kT_lo, K_EXP)], 8: [qk_low(1, qT_hi, qT_lo, Q_EXP)], 9: [y_low]},
                6: {5: [values], 8: [ln_moments(0, s_nl, "nonlin")], 10: [ln_rstd(0)], 15: [residual],
                    17: [ln_moments(1, s_res, "resid")], 20: [ln_rstd(1)], 23: [y_low]},
                7: {2: [swish], 3: [y_low]},
                8: {0: [take_over], 2: [swish], 4: [residual], 5: [ln_moments(0, s_res, "resid")], 6: [ln_rstd(0)]},
                LAST_GATED: {2: [values], 4: [ln_moments(0, s_nl, "nonlin")], 5: [ln_rstd(0)], 8: [residual],
                    10: [ln_moments(1, s_res, "resid")], 11: [ln_rstd(1)], 14: [y_low]},
            }
            at = 0

            def split_low(st):
                dve.wait_ge(s_ahi, PLAIN_BEFORE[st.n] + 1)
                dve.scalar_tensor_tensor(out=slot(a_lo, st).rearrange("p s c -> p (s c)"),
                                         in0=loaded(st).rearrange("p s c -> p (s c)"), scalar=2.0 ** A_EXP,
                                         in1=slot(a_hi, st).rearrange("p s c -> p (s c)"), op0=ALU.mult,
                                         op1=ALU.subtract).then_inc(s_alo, 1)

            def gate_low(u):
                st = STREAM[GATED_FROM + u // SJ]
                dve.wait_ge(s_ghi, u + 1)
                dve.tensor_tensor(slot(a_lo, st)[:, u % SJ, :], gates[:, u % G_RING, :], slot(a_hi, st)[:, u % SJ, :],
                                  ALU.subtract).then_inc(s_glo, 1)

            for st in STREAM:
                if st.p != GATED:
                    at = epilogue(stages, at, freed(st))
                    split_low(st)
                    continue
                for s in range(SJ):
                    u = gated_index(st, s)
                    at = epilogue(stages, at, FIRST_USE[st.n] + s - AHEAD + 1)
                    dve.wait_ge(s_pr, u + 1)
                    if u % ACT_SQUARES == ACT_SQUARES - 1:
                        dve.wait_ge(s_sqa, u // ACT_SQUARES + 1)
                    else:
                        dve.wait_ge(s_sq, u + 1 - u // ACT_SQUARES)
                    dve.scalar_tensor_tensor(out=gates[:, u % G_RING, :], in0=gates[:, u % G_RING, :],
                                             scalar=2.0 ** G_EXP, in1=loaded(st)[:, s, :], op0=ALU.mult,
                                             op1=ALU.mult).then_inc(s_g, 1)
                    if u >= 1:
                        gate_low(u - 1)
                    if u == NB * NC - 1:
                        gate_low(u)
            epilogue(stages, at, THE_END)
            def swish_half(h):
                dve.wait_ge(s_nl, last("nonlin", h + 1))
                dve.scalar_tensor_tensor(out=half_T(xn_T, h), in0=half_T(flat(rows[:, :, :]), h), scalar=b3c[:, 0:1],
                                         in1=half_T(tmp_T, h), op0=ALU.add, op1=ALU.mult).then_inc(s_sw, 1)

            def moments_half(h):
                dve.wait_ge(s_rows, last("rows", 2 if h == 0 else 4))
                dve.tensor_tensor(half(val, h), half(rows, h), half(x_chunk(PASSES, NC - 1), h),
                                  ALU.add).then_inc(s_res, 1)
                dve.wait_ge(s_res, last("resid", h + 1))
                moments_of(range(h * HB, (h + 1) * HB), CB * last("ln", 0) + h * HB)

            def rstd_half(h):
                rstd_of(range(h * HB, (h + 1) * HB), CB * last("ln", 0) + (h + 1) * HB, last("ln", h + 1))

            swish_half(0)
            moments_half(0)
            swish_half(1)
            rstd_half(0)
            moments_half(1)
            rstd_half(1)

        @block.gpsimd
        def _(pool):
            pool.memset(ident[:, :], 0.0).then_inc(s_id0, 1)
            pool.wait_ge(s_id0, 1)
            pool.affine_select(out=ident[:, :], in_=ident[:, :], compare_op=ALU.not_equal, fill=1.0, base=0,
                               pattern=[[-1, P]], channel_multiplier=1).then_inc(s_id, 1)

            def centre(run):
                def go(p, k):
                    pool.wait_ge(s_moments, CB * nth("ln", p, k, run))
                    pool.tensor_tensor(val[:, :, :], val[:, :, :], over_features(moments[:, :, 0]),
                                       ALU.subtract).then_inc(s_cen, 1)
                return go

            def normalise(run):
                def go(p, k):
                    n = nth("ln", p, k, run)
                    pool.wait_ge(s_cen, n)
                    pool.wait_ge(s_newton, 3 * NEWTON * n)
                    pool.tensor_tensor(normalised(p, k, run), val[:, :, :], over_features(stats[:, 1, :]),
                                       ALU.mult).then_inc(s_ln, 1)
                return go

            def store(p, k):
                i = ORDER[p][k]
                pool.wait_ge(s_ln, nth("ln", p, k))
                pool.dma_start(out[:, i * CB:(i + 1) * CB, :], x_chunk(p, k)).then_inc(s_out, 16)

            def affine(p, k):
                pool.wait_ge(s_ln, nth("ln", p, k, 0))
                pool.tensor_tensor(xn[:, :, :], xn[:, :, :], over_blocks(gam), ALU.mult).then_inc(s_aff, 1)
                pool.wait_ge(s_aff, nth("affine", p, k, 0))
                pool.tensor_tensor(xn[:, :, :], xn[:, :, :], over_blocks(bet), ALU.add).then_inc(s_aff, 1)

            stages = {
                4: {3: [centre(0), normalise(0)]},
                5: {3: [centre(0), normalise(0)]},
                6: {8: [centre(0)], 12: [normalise(0)], 13: [affine], 18: [centre(1)], 21: [normalise(1)]},
                8: {5: [centre(0), normalise(0), store]},
                LAST_GATED: {5: [centre(0)], 6: [normalise(0), affine], 11: [centre(1)], 12: [normalise(1)]},
            }
            at = 0

            pool.wait_ge(s_alo, RING)
            for dst, src in small:
                pool.dma_start(dst, src).then_inc(s_small, 16)
            pool.wait_ge(s_alo, STEPS * NC)
            pool.dma_start(x_rows[:, :, :], x).then_inc(s_x, 16)
            for st in STREAM[GATED_FROM:GATED_FROM + STEPS * NC]:
                for s in range(SJ):
                    u = gated_index(st, s)
                    at = epilogue(stages, at, freed(st) + s)
                    if u % ACT_SQUARES == ACT_SQUARES - 1:
                        continue
                    pool.wait_ge(s_a[st.n % LOADS], 16 * (st.n // LOADS + 1))
                    adj_block = loaded(st)[:, s, :]
                    pool.tensor_tensor(adj_block, adj_block, adj_block, ALU.mult).then_inc(s_sq, 1)
            epilogue(stages, at, THE_END)
            for h in range(HALVES):
                blocks, first = slice(h * HB, (h + 1) * HB), ORDER[PASSES][NC - 1] * CB + h * HB
                pool.wait_ge(s_moments, CB * last("ln", 0) + (h + 1) * HB)
                mean, rstd = [v.unsqueeze(2).to_broadcast([P, HB, F])
                              for v in (moments[:, blocks, 0], stats[:, 1, blocks])]
                pool.tensor_tensor(half(val, h), half(val, h), mean, ALU.subtract).then_inc(s_cen, 1)
                pool.wait_ge(s_cen, last("ln", h + 1))
                pool.wait_ge(s_newton, 3 * NEWTON * last("ln", h + 1))
                pool.tensor_tensor(x_rows[:, first:first + HB, :], half(val, h), rstd,
                                   ALU.mult).then_inc(s_ln, 1)


def kernel(**inputs):
    import numpy as np
    import concourse.bacc as bacc
    from concourse.bass_utils import run_bass_kernel_spmd

    def columns(v):
        return np.ascontiguousarray(v.reshape(NB, P).T)

    adj = np.asarray(inputs["adj"])
    x = np.asarray(inputs["x"])
    laid_out = {
        "adj": np.ascontiguousarray(adj.reshape(NC, CH, STEPS, SJ, P).transpose(0, 2, 4, 3, 1)),
        "x": np.ascontiguousarray(x.reshape(NB, P, F).transpose(1, 0, 2)),
        "xt": np.ascontiguousarray(x.T),
        "W1": np.asarray(inputs["L0_gnn_W1"]), "f1": columns(np.asarray(inputs["L0_gnn_f1"])),
        "W2": np.asarray(inputs["L0_gnn_W2"]), "f2": columns(np.asarray(inputs["L0_gnn_f2"])),
        "Wcat": np.asarray(inputs["L1_gnn_weight"]),
        "W_msg": np.asarray(inputs["L2_gnn_W_msg"]), "b_msg": np.asarray(inputs["L2_gnn_b_msg"]),
        "W_qT": np.ascontiguousarray(np.asarray(inputs["L2_gnn_W_q"]).T),
        "W_kT": np.ascontiguousarray(np.asarray(inputs["L2_gnn_W_k"]).T),
        "gate_bias": np.asarray(inputs["L2_gnn_gate_bias"]).reshape(1),
        "W_upd": np.asarray(inputs["L2_gnn_W_upd"]), "b_upd": np.asarray(inputs["L2_gnn_b_upd"]),
        "ln_g": np.asarray(inputs["L2_gnn_ln_gamma"]), "ln_b": np.asarray(inputs["L2_gnn_ln_beta"]),
        "W3": np.asarray(inputs["L3_gnn_W"]), "b3": np.asarray(inputs["L3_gnn_b"]),
    }
    nc = bacc.Bacc("TRN2", target_bir_lowering=False, num_devices=1)
    arrays, args = {}, {}
    for name, a in laid_out.items():
        arrays[f"{name}_dram"] = a
        args[name] = nc.dram_tensor(f"{name}_dram", a.shape, mybir.dt.from_np(a.dtype), kind="ExternalInput").ap()
    args["out"] = nc.dram_tensor("out_dram", (P, NB, F), F32, kind="ExternalOutput").ap()
    build(nc, **args)
    r = run_bass_kernel_spmd(nc, [arrays], core_ids=[0])
    return np.ascontiguousarray(r.results[0]["out_dram"].transpose(1, 0, 2)).reshape(N, F)
```
